# Optimizing a Trainium2 kernel written in Bass

```python
import numpy as np
import jax
import jax.numpy as jnp

def _softmax(x, axis=-1):
    return jax.nn.softmax(x, axis=axis)

def _gelu(x):
    return jax.nn.gelu(x, approximate=True)

def _silu(x):
    return jax.nn.silu(x)

def _sigmoid(x):
    return jax.nn.sigmoid(x)

def _layernorm(x, axis=-1, eps=1e-05):
    m = jnp.mean(x, axis=axis, keepdims=True)
    v = jnp.var(x, axis=axis, keepdims=True)
    return (x - m) / jnp.sqrt(v + eps)

def _scatter_add(tgt, idx, src, axis=0):
    return tgt.at[idx].add(src)

def _segment_sum(src, seg, n):
    return jax.ops.segment_sum(src, seg, n)
kernel_name = 'mk_adj_resnorm_d2_adj_r2_e45fdf'

def setup_inputs(seed: int=0):
    np.random.seed(seed)
    _w = jnp.asarray

    def _rec_inputs():
        import jax
        import jax.numpy as jnp
        _gk = jax.random.key(seed)
        x = -0.001547 + 1.001 * jax.random.normal(jax.random.fold_in(_gk, 1), (64, 128, 128), jnp.float32)
        _a = jax.random.bernoulli(jax.random.fold_in(_gk, 2), 0.015625, (64, 128, 128))
        _a = jnp.logical_or(_a, jnp.swapaxes(_a, -1, -2))
        _a = jnp.logical_or(_a, jnp.eye(128, dtype=bool))
        _af = _a.astype(jnp.float32)
        _af = _af * jax.random.uniform(jax.random.fold_in(_gk, 3), (64, 128, 128), jnp.float32, 0.05, 5.99996)
        adj = _af
        return (x, adj)
    x, adj = _rec_inputs()

    def _L0_gnn_setup():
        import jax, jax.numpy as jnp
        import numpy as np
        import math
        CUTOFF = 5.0
        LOG2 = math.log(2.0)

        def ssp(x):
            return jax.nn.softplus(x) - LOG2
        key = jax.random.key(seed)
        ks = jax.random.split(key, 12)
        B, A, C, F, R = (4, 256, 128, 128, 20)
        x = jax.random.normal(ks[0], (B, A, C), dtype=jnp.float32)
        d_ij = jax.random.uniform(ks[1], (B, A, A), dtype=jnp.float32) * 6.0
        widths = jnp.linspace(1.0, CUTOFF, R, dtype=jnp.float32)
        offsets = jnp.zeros((R,), dtype=jnp.float32)
        s = lambda k, shp: jax.random.normal(k, shp, dtype=jnp.float32) * 0.05
        w_in2f = s(ks[2], (C, F))
        fw1, fb1 = (s(ks[3], (R, F)), jnp.zeros((F,), jnp.float32))
        fw2, fb2 = (s(ks[4], (F, F)), jnp.zeros((F,), jnp.float32))
        ow1, ob1 = (s(ks[5], (F, C)), jnp.zeros((C,), jnp.float32))
        ow2, ob2 = (s(ks[6], (C, C)), jnp.zeros((C,), jnp.float32))
        return dict(x=x, d_ij=d_ij, widths=widths, offsets=offsets, w_in2f=w_in2f, fw1=fw1, fb1=fb1, fw2=fw2, fb2=fb2, ow1=ow1, ob1=ob1, ow2=ow2, ob2=ob2)
    _L0_gnn_all = _L0_gnn_setup()
    _L0_gnn_in = {k: v for k, v in _L0_gnn_all.items() if k in ('widths', 'offsets', 'w_in2f', 'fw1', 'fb1', 'fw2', 'fb2', 'ow1', 'ob1', 'ow2', 'ob2')}
    del _L0_gnn_all

    def _L1_gnn_setup():
        import jax, jax.numpy as jnp
        import numpy as np
        B, N, FIN, FOUT = (32, 512, 128, 128)
        NEG_SLOPE = 0.01
        key = jax.random.key(seed)
        k1, k2, k3, k4 = jax.random.split(key, 4)
        node_mat = jax.random.normal(k1, (B, N, FIN), dtype=jnp.float32)
        adj_mat = jax.random.uniform(k2, (B, N, N), dtype=jnp.float32)
        bound = 1.0 / np.sqrt(FIN)
        W = jax.random.uniform(k3, (FOUT, FIN), minval=-bound, maxval=bound, dtype=jnp.float32)
        b = jax.random.uniform(k4, (FOUT,), minval=-bound, maxval=bound, dtype=jnp.float32)
        return {'node_mat': node_mat, 'adj_mat': adj_mat, 'W': W, 'b': b}
    _L1_gnn_all = _L1_gnn_setup()
    _L1_gnn_in = {k: v for k, v in _L1_gnn_all.items() if k in ('W', 'b')}
    del _L1_gnn_all
    return {'x': x, 'adj': adj, 'L0_gnn_widths': _L0_gnn_in['widths'], 'L0_gnn_offsets': _L0_gnn_in['offsets'], 'L0_gnn_w_in2f': _L0_gnn_in['w_in2f'], 'L0_gnn_fw1': _L0_gnn_in['fw1'], 'L0_gnn_fb1': _L0_gnn_in['fb1'], 'L0_gnn_fw2': _L0_gnn_in['fw2'], 'L0_gnn_fb2': _L0_gnn_in['fb2'], 'L0_gnn_ow1': _L0_gnn_in['ow1'], 'L0_gnn_ob1': _L0_gnn_in['ob1'], 'L0_gnn_ow2': _L0_gnn_in['ow2'], 'L0_gnn_ob2': _L0_gnn_in['ob2'], 'L1_gnn_W': _L1_gnn_in['W'], 'L1_gnn_b': _L1_gnn_in['b']}

def reference(x, adj, L0_gnn_widths, L0_gnn_offsets, L0_gnn_w_in2f, L0_gnn_fw1, L0_gnn_fb1, L0_gnn_fw2, L0_gnn_fb2, L0_gnn_ow1, L0_gnn_ob1, L0_gnn_ow2, L0_gnn_ob2, L1_gnn_W, L1_gnn_b):
    import jax
    import jax.numpy as jnp

    def _L0_gnn_ref(x, d_ij, widths, offsets, w_in2f, fw1, fb1, fw2, fb2, ow1, ob1, ow2, ob2):
        import jax, jax.numpy as jnp
        import numpy as np
        import math
        CUTOFF = 5.0
        LOG2 = math.log(2.0)

        def ssp(x):
            return jax.nn.softplus(x) - LOG2
        coeff = -0.5 / (widths * widths)
        diff = d_ij[..., None] - offsets
        f_ij = jnp.exp(coeff * diff * diff)
        rcut = 0.5 * (jnp.cos(d_ij * (math.pi / CUTOFF)) + 1.0) * (d_ij < CUTOFF).astype(d_ij.dtype)
        y = x @ w_in2f
        W = ssp(f_ij @ fw1 + fb1) @ fw2 + fb2
        W = W * rcut[..., None]
        agg = jnp.einsum('bjf,bijf->bif', y, W)
        out = ssp(agg @ ow1 + ob1) @ ow2 + ob2
        return out

    def _L1_gnn_ref(node_mat, adj_mat, W, b):
        import jax, jax.numpy as jnp
        import numpy as np
        B, N, FIN, FOUT = (32, 512, 128, 128)
        NEG_SLOPE = 0.01
        n_neighbors = adj_mat.sum(axis=-1, keepdims=True)
        norm_adj = adj_mat / n_neighbors
        agg = jnp.einsum('bnm,bmf->bnf', norm_adj, node_mat)
        out = jnp.einsum('bnf,of->bno', agg, W) + b
        return jnp.where(out >= 0, out, NEG_SLOPE * out)
    x = _layernorm(x + _L0_gnn_ref(x, adj, L0_gnn_widths, L0_gnn_offsets, L0_gnn_w_in2f, L0_gnn_fw1, L0_gnn_fb1, L0_gnn_fw2, L0_gnn_fb2, L0_gnn_ow1, L0_gnn_ob1, L0_gnn_ow2, L0_gnn_ob2), axis=-1)
    x = _layernorm(x + _L1_gnn_ref(x, adj, L1_gnn_W, L1_gnn_b), axis=-1)
    return x

_drawn_inputs = setup_inputs


def setup_inputs(seed=0):
    import zlib

    import numpy as np

    out = dict(_drawn_inputs(seed))
    spreads = {'L0_gnn_offsets': (0.0, 0.1),
     'L0_gnn_fb1': (0.0, 0.1),
     'L0_gnn_fb2': (0.0, 0.1),
     'L0_gnn_ob1': (0.0, 0.1),
     'L0_gnn_ob2': (0.0, 0.1)}
    factors = {}
    for name, (base, spread) in spreads.items():
        noise = np.random.default_rng([zlib.crc32(name.encode()), seed]).standard_normal(out[name].shape)
        drawn = base * np.exp(spread * noise) if base else spread * noise
        out[name] = jnp.asarray(drawn.astype(out[name].dtype))
    for name, factor in factors.items():
        out[name] = (out[name] * factor).astype(out[name].dtype)
    return out
```

```python
import math
from contextlib import ExitStack

import concourse.bass as bass
from concourse import mybir

F32 = mybir.dt.float32
BF16 = mybir.dt.bfloat16
U32 = mybir.dt.uint32
I32 = mybir.dt.int32
ALU = mybir.AluOpType
ACT = mybir.ActivationFunctionType
AX = mybir.AxisListType

B, N, C, R = 64, 128, 128, 20
PAIRS = B // 2
G = 2
MAIN = 5
SLOTS = G * (MAIN + 1)
GROUPS, PER = SLOTS // 4, 4
RING = 3
CUTOFF = 5.0
LN2 = math.log(2.0)
CLAMP = 40.0
EPS = 1e-5
MAGIC = 1.5 * 2.0 ** 23
COS = [(-1.0) ** k * (math.pi / 10) ** (2 * k) / math.factorial(2 * k) for k in range(8)]
GRAPH_OF = [0, 0, 0, 0, 0, 0, 1, 1, 1, 1, 1, 1]


def build(nc, x, xT, adjT, widths, offsets, w_in2f, fw1, fw1T, fb1, fw2, fb2, ow1, ob1, ow2, ob2, WT, bL, out):
    ctx = ExitStack()
    with ctx:
        def sb(name, shape, dt=F32):
            return ctx.enter_context(nc.sbuf_tensor(name, shape, dt))

        def pb(name, shape):
            return ctx.enter_context(nc.psum_tensor(name, shape, F32))

        def sem(name):
            return ctx.enter_context(nc.semaphore(name))

        iota_i = sb("iota_i", [N, N], I32)
        part_i = sb("part_i", [N, 1], I32)
        iota = sb("iota", [N, N])
        part = sb("part", [N, 1])
        part5 = sb("part5", [N, 1])
        ident = sb("ident", [N, N])
        upper = sb("upper", [N, N])
        ones = sb("ones", [N, N])
        ones_h = sb("ones_h", [N, N], BF16)
        win = sb("win", [C, C])
        fw1s = sb("fw1s", [N, C])
        fw2s = sb("fw2s", [C, C])
        ow1s = sb("ow1s", [C, C])
        ow2s = sb("ow2s", [C, C])
        WTs = sb("WTs", [C, C])
        cols = sb("cols", [C, 8])
        FB1, OB1, FB1L, OB1L, EPSC = (cols[:, i:i + 1] for i in range(5))
        width_c = sb("width_c", [N, 1])
        noff_c = sb("noff_c", [N, 1])
        coef_c = sb("coef_c", [N, 1])
        b2_bc = sb("b2_bc", [N, C])
        ob2_bc = sb("ob2_bc", [N, C])
        bL_bc = sb("bL_bc", [N, C])
        b2_hi = sb("b2_hi", [N, C], BF16)
        b2_mid = sb("b2_mid", [N, C], BF16)
        b2_res = sb("b2_res", [N, C])
        b2_sel = sb("b2_sel", [N, C])
        b2_rows = sb("b2_rows", [N, PER, C], BF16)
        W0_bc = sb("W0_bc", [N, C])
        f0 = sb("f0", [N, 2])
        s0 = sb("s0", [C, 4])
        hsum = sb("hsum", [C, R + 1])

        ADJ = sb("ADJ", [N, RING, G * N])
        XT = sb("XT", [C, RING, G * N])
        KEY = sb("KEY", [N, G, N])
        KEY2 = sb("KEY2", [N, G, N])
        IDX = sb("IDX", [N, G, 16], U32)
        TAB = sb("TAB", [N, RING, G, 34])
        over = sb("over", [N, G, 16 - MAIN])
        cnt = sb("cnt", [N, RING, G])
        end = sb("end", [N, G])
        SEL = sb("SEL", [N, G, N])
        SELa = sb("SELa", [N, G, N])
        OVT = sb("OVT", [N, G, 34])
        rel = sb("rel", [N, G])
        mask = sb("mask", [N, G, 16])
        picked = sb("picked", [N, G, 2, 16])
        SV = sb("SV", [N, RING, 2, SLOTS])
        RC = sb("RC", [N, RING, SLOTS])
        VB = sb("VB", [N, SLOTS, 32])
        usq = sb("usq", [N, SLOTS])
        acc = sb("acc", [N, SLOTS])
        live = sb("live", [N, SLOTS])
        Y = sb("Y", [N, RING, 2 * G, C])
        M0 = sb("M0", [N, RING, G * N])
        YW0 = sb("YW0", [N, RING, G, C])
        SQ = sb("SQ", [N, GROUPS * N])
        FT = sb("FT", [N, RING, GROUPS * N])
        negs = sb("negs", [N, G * N])
        news = sb("news", [N, 8])
        flags = sb("flags", [N, 8])
        E = sb("E", [C, PER, GROUPS * N])
        S = sb("S", [C, RING, PER, GROUPS * N])
        P = sb("P", [N, GROUPS, PER * C])
        OH = sb("OH", [N, SLOTS, N])
        AGG = sb("AGG", [C, G * N])
        X = sb("X", [N, RING, G * C])
        XB = sb("XB", [N, RING, G * C])
        HM = sb("HM", [C, G * N])
        L2 = sb("L2", [C, G * N])
        S2 = sb("S2", [C, G * N])
        Z = sb("Z", [N, G * C])
        st = sb("st", [N, 2, G, 6])
        mv = sb("mv", [N, 2, G, 2])
        lnv = sb("lnv", [N, 2, G])
        rstd = sb("rstd", [N, 2, G])
        X1 = sb("X1", [N, RING, G * C])
        ADJ2 = sb("ADJ2", [N, RING, G * N])
        A2 = sb("A2", [C, G * N])
        rn = sb("rn", [N, G])
        U = sb("U", [N, G * C])
        V = sb("V", [N, G * C])
        Z2 = sb("Z2", [N, G * C])
        OUT = sb("OUT", [N, RING, G * C])
        g_rc = sb("g_rc", [N, G * N])
        g_k = sb("g_k", [N, G * N])
        g_u = sb("g_u", [N, G * N])
        g_val = sb("g_val", [N, PER])
        g_vb = sb("g_vb", [N, PER, 32])
        g_idx = sb("g_idx", [N, PER])
        g_w = sb("g_w", [N, PER])
        flag1 = sb("flag1", [N, 1])
        flag2 = sb("flag2", [N, 1])
        flag_i = sb("flag_i", [1, 1], I32)

        H = pb("H", [N, PER, 512])
        Wb = pb("Wb", [N, PER * C])
        AG = pb("AG", [N, 512])
        M = pb("M", [N, 512])
        O = pb("O", [N, 512])
        HH = H[:, :, 0:GROUPS * N]
        T1, T2, T3, T4 = (H[:, k, 0:G * N].rearrange("p (g c) -> p g c", g=G) for k in range(4))
        RANK = M[:, 504:506]
        GY = O[:, 0:G * C]
        GT = O[:, 256:256 + G * 34].rearrange("p (g c) -> p g c", g=G)
        NS = H[:, 3, G * C:G * C + G]

        def pair(t):
            return t.rearrange("p (g c) -> p g c", g=G)

        c_dma = sem("c_dma")
        pool_consts = sem("pool_consts")
        v_consts = sem("v_consts")
        v_c1 = sem("v_c1")
        v_c2 = sem("v_c2")
        a_c1 = sem("a_c1")
        a_c2 = sem("a_c2")
        pe_c1 = sem("pe_c1")
        pe_c2 = sem("pe_c2")
        v_setup = sem("v_setup")
        loadA = [sem(f"loadA{r}") for r in range(RING)]
        loadX = [sem(f"loadX{r}") for r in range(RING)]
        loadD = [sem(f"loadD{r}") for r in range(RING)]
        stored = [sem(f"stored{r}") for r in range(RING)]
        names = ("key_ready cnt_ready rank_mm rank_read sel_ready y_mm y_ready gather_mm yo_ready ovt_ready slots_ready vb_ready "
                 "m0_ready yw0_ready rc_ready bcast_mm sq_ready f_ready neg_ready h_mm e_ready s_ready "
                 "agg_mm agg_ready ow1_mm hm_ready l2_ready s2_ready ow2_mm xb_ready z_ready mv1_ready rs1_ready "
                 "x1_ready a2_mm ns_mm a2_ready out_mm u_ready v_ready z2_ready mv2_ready rs2_ready out_ready").split()
        s = {k: sem(k) for k in names}
        w_mm = [sem(f"w_mm{g}") for g in range(GROUPS)]
        p_ready = [sem(f"p_ready{g}") for g in range(GROUPS)]
        oh_ready = [sem(f"oh_ready{g}") for g in range(GROUPS)]
        scat_mm = [sem(f"scat_mm{g}") for g in range(GROUPS)]
        flag_v = sem("flag_v")
        flag_pe = sem("flag_pe")
        flag_ready = sem("flag_ready")
        g_load = sem("g_load")
        g_stored = sem("g_stored")
        g_pair_done = sem("g_pair_done")
        gnames = ("rc y_mm y_ready pick bcast f h_mm hm l s w_mm p scat add agg "
                  "ow1_mm hm_ready l2_ready s2_ready ow2_mm z_ready mv1_ready rs1_ready xb_ready "
                  "x1_ready a2_mm ns_mm a2_ready out_mm u_ready v_ready z2_ready mv2_ready rs2_ready out_ready").split()
        gs = {k: sem("g_" + k) for k in gnames}

        def wait(eng, which, value):
            if not isinstance(value, int) or value > 0:
                eng.wait_ge(which, value)

        block = ctx.enter_context(nc.Block())

        LAG = {"A": 0, "B1": 1, "B2": 2, "C1": 3, "C2": 4}
        AHEAD = 2

        def steps(eng, step, lag=LAG["C2"]):
            first = lag + 1
            rolls = (PAIRS - first) // RING
            for t in range(first):
                step(t, t // RING, t % RING)
            with eng.Fori(0, rolls) as q:
                for k in range(RING):
                    c = first + k
                    step(q * RING + c, q + c // RING, c % RING)
            for t in range(first + RING * rolls, PAIRS + lag):
                step(t, t // RING, t % RING)

        def on(t, stage):
            return not isinstance(t, int) or 0 <= t - LAG[stage] < PAIRS

        def turn(cyc, r, lag):
            return cyc + (r - lag) // RING, (r - lag) % RING

        def load_a(sp, n, r):
            wait(sp, s["key_ready"], n - 2)
            wait(sp, s["y_mm"], n - 2)
            wait(sp, s["m0_ready"], n - 2)
            wait(sp, s["neg_ready"], n - 2)
            sp.dma_start(ADJ[:, r, :], adjT[n]).then_inc(loadA[r], 16)
            sp.dma_start(XT[:, r, :], xT[n]).then_inc(loadA[r], 16)

        def load_x(sp, n, r):
            wait(sp, s["xb_ready"], n - 2)
            sp.dma_start(X[:, r, :], x[n]).then_inc(loadX[r], 16)

        def load_d(sp, n, r):
            wait(sp, s["ns_mm"], n - 2)
            sp.dma_start(ADJ2[:, r, :], adjT[n]).then_inc(loadD[r], 16)

        @block.sync
        def _(sp):
            sp.wait_ge(v_consts, 1)
            for t in range(4):
                sp.dma_start(fw1s[32 * t:32 * t + R, :], fw1).then_inc(c_dma, 16)
                sp.dma_start(width_c[32 * t:32 * t + R, :], widths).then_inc(c_dma, 16)
                sp.dma_start(noff_c[32 * t:32 * t + R, :], offsets).then_inc(c_dma, 16)
            for dst, src in ((win, w_in2f), (fw2s, fw2), (ow1s, ow1), (ow2s, ow2), (WTs, WT)):
                sp.dma_start(dst[:], src).then_inc(c_dma, 16)
            sp.dma_start(FB1, fb1).then_inc(c_dma, 16)
            sp.dma_start(OB1, ob1).then_inc(c_dma, 16)
            for dst, src in ((b2_bc, fb2), (ob2_bc, ob2), (bL_bc, bL)):
                sp.dma_start(dst[:], src.partition_broadcast(N)).then_inc(c_dma, 16)
            sp.dma_start(hsum[:, 0:R], fw1T).then_inc(c_dma, 16)

            def step(t, cyc, r):
                def has(lag):
                    return not isinstance(t, int) or 0 <= t - lag < PAIRS

                if has(0):
                    load_a(sp, t, r)
                if has(LAG["C1"]):
                    load_x(sp, t - LAG["C1"], turn(cyc, r, LAG["C1"])[1])
                if has(LAG["C2"]):
                    load_d(sp, t - LAG["C2"], turn(cyc, r, LAG["C2"])[1])
                lag = LAG["C2"] + AHEAD
                if has(lag):
                    rr = turn(cyc, r, lag)[1]
                    wait(sp, s["out_ready"], t - lag + 1)
                    sp.dma_start(out[t - lag], OUT[:, rr, :]).then_inc(stored[rr], 16)

            steps(sp, step, LAG["C2"] + AHEAD)
            for r in range(RING):
                sp.wait_ge(stored[r], 16 * ((PAIRS - r + RING - 1) // RING))
            sp.wait_ge(flag_ready, 1)
            general = sp.value_load(flag_i[0:1, 0:1], min_val=0, max_val=1)
            with sp.If(general > 0):
                with sp.Fori(0, PAIRS) as n:
                    sp.dma_start(ADJ[:, 0, :], adjT[n]).then_inc(g_load, 16)
                    sp.dma_start(ADJ2[:, 0, :], adjT[n]).then_inc(g_load, 16)
                    sp.dma_start(XT[:, 0, :], xT[n]).then_inc(g_load, 16)
                    sp.dma_start(X[:, 0, :], x[n]).then_inc(g_load, 16)
                    sp.wait_ge(gs["out_ready"], n + 1)
                    sp.dma_start(out[n], OUT[:, 0, :]).then_inc(g_stored, 16)
                    sp.wait_ge(g_stored, n * 16 + 16)
                    sp.sem_inc(g_pair_done, 1)
                sp.nop()

        @block.gpsimd
        def _(pool):
            nc.gpsimd.iota(iota_i[:], pattern=[[1, N]], base=0, channel_multiplier=0).then_inc(pool_consts, 1)
            nc.gpsimd.iota(part_i[:], pattern=[[1, 1]], base=0, channel_multiplier=1).then_inc(pool_consts, 1)
            pool.wait_ge(v_setup, 1)

            def step(t, cyc, r):
                if on(t, "C1"):
                    c, rr = turn(cyc, r, 3)
                    wait(pool, loadX[rr], c * 16 + 16)
                    nc.gpsimd.tensor_tensor(pair(XB[:, rr, :]), pair(X[:, rr, :]),
                                            ob2_bc[:].unsqueeze(1).broadcast_to([N, G, C]), ALU.add).then_inc(s["xb_ready"], 1)
                if on(t, "A"):
                    wait(pool, s["y_ready"], t + 1)
                    nc.gpsimd.tensor_tensor(YW0[:, r, :, :], Y[:, r, 0:2 * G:2, :],
                                            W0_bc[:].unsqueeze(1).broadcast_to([N, G, C]), ALU.mult).then_inc(s["yw0_ready"], 1)
                if on(t, "C2"):
                    rr = turn(cyc, r, 4)[1]
                    wait(pool, s["v_ready"], t - 3)
                    wait(pool, s["mv2_ready"], t - 4)
                    nc.gpsimd.tensor_tensor(Z2[:], V[:], X1[:, rr, :], ALU.add).then_inc(s["z2_ready"], 1)
                if on(t, "A"):
                    wait(pool, s["slots_ready"], t + 1)
                    val = SV[:, r, 0, :]
                    nc.gpsimd.tensor_tensor(usq[:], val, val, ALU.mult)
                    nc.gpsimd.tensor_scalar(live[:], val, 0.0, None, ALU.is_gt)
                    nc.gpsimd.drain()
                    nc.gpsimd.tensor_scalar(acc[:], usq[:], COS[7], COS[6], ALU.mult, ALU.add)
                    for k in range(5, -1, -1):
                        nc.gpsimd.drain()
                        nc.gpsimd.tensor_tensor(acc[:], acc[:], usq[:], ALU.mult)
                        nc.gpsimd.drain()
                        nc.gpsimd.tensor_scalar(acc[:], acc[:], 1.0, COS[k], ALU.mult, ALU.add)
                    nc.gpsimd.drain()
                    nc.gpsimd.tensor_tensor(acc[:], acc[:], acc[:], ALU.mult)
                    nc.gpsimd.drain()
                    nc.gpsimd.tensor_tensor(RC[:, r, :], acc[:], live[:], ALU.mult).then_inc(s["rc_ready"], 1)
                    nc.gpsimd.drain()

            steps(pool, step)

        def act_c1_softplus(act, q, n):
            act.wait_ge(q["hm_ready"], n + 1)
            nc.scalar.activation(L2[:], HM[:], ACT.Exp)
            nc.scalar.drain()
            nc.scalar.activation(L2[:], L2[:], ACT.Ln, bias=0.5, scale=0.5).then_inc(q["l2_ready"], 1)

        def act_rstd(act, ready, done, n, k):
            act.wait_ge(ready, n + 1)
            nc.scalar.activation(lnv[:, k, :], mv[:, k, :, 1], ACT.Ln, bias=EPSC)
            nc.scalar.drain()
            nc.scalar.activation(rstd[:, k, :], lnv[:, k, :], ACT.Exp, scale=-0.5).then_inc(done, 1)

        def act_a2(act, q, n):
            act.wait_ge(q["a2_mm"], n + 1)
            nc.scalar.copy(pair(A2[:]), T3).then_inc(q["a2_ready"], 1)

        @block.scalar
        def _(act):
            nc.scalar.preload_act_table_set("natural_log_exp_and_others")
            act.wait_ge(v_c1, 1)
            nc.scalar.activation(f0[:, 0:1], noff_c[:], ACT.Square)
            nc.scalar.drain()
            nc.scalar.activation(f0[:, 1:2], f0[:, 0:1], ACT.Exp, scale=coef_c[:, 0:1]).then_inc(a_c1, 1)
            act.wait_ge(v_c2, 1)
            nc.scalar.activation(s0[:, 1:2], s0[:, 0:1], ACT.Exp)
            nc.scalar.drain()
            nc.scalar.activation(s0[:, 2:3], s0[:, 1:2], ACT.Ln, bias=0.5, scale=0.5).then_inc(a_c2, 1)

            def step(t, cyc, r):
                if on(t, "A"):
                    act.wait_ge(loadA[r], cyc * 32 + 32)
                    wait(act, s["rank_read"], t)
                    nc.scalar.activation(negs[:], ADJ[:, r, :], ACT.Relu, scale=-1.0,
                                         accum_out=news[:, 0:1]).then_inc(s["neg_ready"], 1)
                    act.wait_ge(s["y_mm"], t + 1)
                    wait(act, p_ready[2], t - 2)
                    nc.scalar.copy(Y[:, r, 0:2 * G:2, :], pair(M[:, 0:G * C])).then_inc(s["y_ready"], 1)
                if on(t, "B1"):
                    rr = turn(cyc, r, 1)[1]
                    act.wait_ge(s["h_mm"], t)
                    nc.scalar.activation(E[:], HH, ACT.Exp, bias=FB1).then_inc(s["e_ready"], 1)
                    nc.scalar.drain()
                    nc.scalar.activation(S[:, rr, :, :], E[:], ACT.Ln, bias=0.5, scale=0.5).then_inc(s["s_ready"], 1)
                if on(t, "C1"):
                    act_c1_softplus(act, s, t - 3)
                if on(t, "C2"):
                    act_a2(act, s, t - 4)
                if on(t, "A"):
                    act.wait_ge(s["gather_mm"], t + 1)
                    wait(act, s["slots_ready"], t)
                    nc.scalar.copy(OVT[:], GT).then_inc(s["ovt_ready"], 1)
                    nc.scalar.copy(Y[:, r, 1:2 * G:2, :], pair(GY)).then_inc(s["yo_ready"], 1)
                if on(t, "C1"):
                    act_rstd(act, s["mv1_ready"], s["rs1_ready"], t - 3, 0)
                if on(t, "A"):
                    act.wait_ge(s["bcast_mm"], t + 1)
                    nc.scalar.activation(SQ[:], M[:, 0:GROUPS * N], ACT.Square, bias=noff_c[:, 0:1]).then_inc(s["sq_ready"], 1)
                    nc.scalar.drain()
                    nc.scalar.activation(FT[:, r, :], SQ[:], ACT.Exp, scale=coef_c[:, 0:1]).then_inc(s["f_ready"], 1)
                if on(t, "C2"):
                    act_rstd(act, s["mv2_ready"], s["rs2_ready"], t - 4, 1)
                if on(t, "B2"):
                    act.wait_ge(s["agg_mm"], t - 1)
                    wait(act, s["ow1_mm"], t - 2)
                    nc.scalar.copy(AGG[:], AG[:, 0:G * N]).then_inc(s["agg_ready"], 1)

            steps(act, step)

            act.wait_ge(flag_ready, 1)
            general = act.value_load(flag_i[0:1, 0:1], min_val=0, max_val=1)
            with act.If(general > 0):
                with act.Fori(0, PAIRS) as n:
                    for g in range(G):
                        act.wait_ge(gs["y_mm"], n * 2 + (g + 1))
                        nc.scalar.copy(Y[:, 0, 0, :], M[:, 0:C]).then_inc(gs["y_ready"], 1)
                        with act.Fori(0, N // PER) as i:
                            m = n * (G * N // PER) + i + g * (N // PER)
                            act.wait_ge(gs["bcast"], m + 1)
                            nc.scalar.activation(SQ[:, 0:N], M[:, 0:N], ACT.Square, bias=noff_c[:, 0:1])
                            nc.scalar.drain()
                            nc.scalar.activation(FT[:, 0, 0:N], SQ[:, 0:N], ACT.Exp, scale=coef_c[:, 0:1]).then_inc(gs["f"], 1)
                            act.wait_ge(gs["hm"], m + 1)
                            nc.scalar.activation(E[:, :, 0:N], E[:, :, 0:N], ACT.Exp)
                            nc.scalar.drain()
                            nc.scalar.activation(E[:, :, 0:N], E[:, :, 0:N], ACT.Ln, bias=0.5, scale=0.5).then_inc(gs["l"], 1)
                    act_c1_softplus(act, gs, n)
                    act_rstd(act, gs["mv1_ready"], gs["rs1_ready"], n, 0)
                    act_a2(act, gs, n)
                    act_rstd(act, gs["mv2_ready"], gs["rs2_ready"], n, 1)
                act.nop()

        def v_c1_min(v, q, n):
            v.wait_ge(q["ow1_mm"], n + 1)
            nc.vector.tensor_scalar(pair(HM[:]), T1, OB1, CLAMP, ALU.add, ALU.min).then_inc(q["hm_ready"], 1)

        def v_c1_max(v, q, n):
            v.wait_ge(q["l2_ready"], n + 1)
            nc.vector.scalar_tensor_tensor(pair(S2[:]), T1, OB1L, pair(L2[:]), ALU.add, ALU.max).then_inc(q["s2_ready"], 1)

        def v_stats(src, k, done):
            for g in range(G):
                nc.vector.bn_stats(st[:, k, g, :], src[:, g * C:(g + 1) * C])
            nc.vector.drain()
            for g in range(G):
                last = nc.vector.bn_aggr(mv[:, k, g, :], st[:, k, g, :])
            last.then_inc(done, 1)

        def v_c1_residual(v, q, n, rr):
            v.wait_ge(q["ow2_mm"], n + 1)
            v.wait_ge(q["xb_ready"], n + 1)
            nc.vector.tensor_tensor(pair(Z[:]), T2, pair(XB[:, rr, :]), ALU.add).then_inc(q["z_ready"], 1)
            nc.vector.drain()
            v_stats(Z, 0, q["mv1_ready"])

        def v_norm(v, ready, done, n, k, src, dst):
            v.wait_ge(ready, n + 1)
            for g in range(G):
                last = nc.vector.tensor_scalar(dst[:, g * C:(g + 1) * C], src[:, g * C:(g + 1) * C],
                                               mv[:, k, g, 0:1], rstd[:, k, g:g + 1], ALU.subtract, ALU.mult)
            last.then_inc(done, 1)

        def v_c2_act(v, q, n):
            v.wait_ge(q["out_mm"], n + 1)
            nc.vector.reciprocal(rn[:], NS)
            nc.vector.drain()
            for g in range(G):
                last = nc.vector.scalar_tensor_tensor(U[:, g * C:(g + 1) * C], T4[:, g, :], rn[:, g:g + 1], bL_bc[:],
                                                      ALU.mult, ALU.add)
            last.then_inc(q["u_ready"], 1)
            nc.vector.drain()
            nc.vector.scalar_tensor_tensor(V[:], U[:], 0.01, U[:], ALU.mult, ALU.max).then_inc(q["v_ready"], 1)

        def one_hot(q, idx, w):
            return nc.vector.tensor_scalar(OH[:, q, :], iota[:], idx, w, ALU.is_equal, ALU.mult)

        @block.vector
        def _(v):
            nc.vector.memset(width_c[:], 1.0)
            nc.vector.memset(noff_c[:], 0.0)
            nc.vector.memset(ones[:], 1.0)
            nc.vector.memset(ones_h[:], 1.0)
            nc.vector.memset(flags[:], 0.0)
            nc.vector.memset(news[:], 0.0)
            nc.vector.memset(TAB[:].rearrange("p a b c -> p (a b c)"), 0.0)
            nc.vector.memset(EPSC, EPS)
            nc.vector.drain().then_inc(v_consts, 1)
            v.wait_ge(pool_consts, 2)
            nc.vector.tensor_copy(iota[:], iota_i[:])
            nc.vector.tensor_copy(part[:], part_i[:])
            nc.vector.drain()
            nc.vector.tensor_scalar(ident[:], iota[:], part[:, 0:1], None, ALU.is_equal)
            nc.vector.tensor_scalar(upper[:], iota[:], part[:, 0:1], None, ALU.is_gt)
            nc.vector.tensor_scalar(part5[:], part[:], float(MAIN), None, ALU.add)
            v.wait_ge(c_dma, 16 * 23)
            nc.vector.tensor_scalar(noff_c[:], noff_c[:], -1.0, None, ALU.mult)
            nc.vector.tensor_tensor(width_c[:], width_c[:], width_c[:], ALU.mult)
            nc.vector.tensor_scalar(FB1L, FB1, LN2, None, ALU.subtract)
            nc.vector.tensor_scalar(OB1L, OB1, LN2, None, ALU.subtract)
            nc.vector.tensor_copy(hsum[:, R:R + 1], FB1)
            nc.vector.drain()
            nc.vector.reciprocal(coef_c[:], width_c[:])
            nc.vector.drain()
            nc.vector.tensor_scalar(coef_c[:], coef_c[:], -0.5, None, ALU.mult).then_inc(v_c1, 1)
            nc.vector.tensor_reduce(s0[:, 3:4], hsum[:], AX.X, ALU.add, apply_absolute_value=True)
            nc.vector.tensor_copy(b2_hi[:], b2_bc[:])
            nc.vector.drain()
            nc.vector.tensor_scalar(flags[:, 7:8], s0[:, 3:4], CLAMP, None, ALU.subtract)
            nc.vector.tensor_tensor(b2_res[:], b2_bc[:], b2_hi[:], ALU.subtract)
            nc.vector.drain()
            nc.vector.tensor_copy(b2_mid[:], b2_res[:])
            nc.vector.drain()
            nc.vector.tensor_tensor(b2_res[:], b2_res[:], b2_mid[:], ALU.subtract)
            nc.vector.tensor_scalar(b2_sel[:], b2_hi[:], ident[:, 0:1], None, ALU.mult)
            nc.vector.drain()
            nc.vector.scalar_tensor_tensor(b2_sel[:], b2_mid[:], ident[:, 1:2], b2_sel[:], ALU.mult, ALU.add)
            nc.vector.drain()
            nc.vector.scalar_tensor_tensor(b2_sel[:], b2_res[:], ident[:, 2:3], b2_sel[:], ALU.mult, ALU.add)
            nc.vector.drain()
            for t in range(PER):
                nc.vector.tensor_copy(b2_rows[:, t, :], b2_sel[:])
            v.wait_ge(pe_c1, 1)
            nc.vector.tensor_scalar(s0[:, 0:1], M[:, 0:1], FB1, CLAMP, ALU.add, ALU.min).then_inc(v_c2, 1)
            v.wait_ge(a_c2, 1)
            nc.vector.scalar_tensor_tensor(s0[:, 3:4], M[:, 0:1], FB1L, s0[:, 2:3], ALU.add, ALU.max)
            nc.vector.drain()
            nc.vector.tensor_scalar(S2[:, 0:N], ones[:], s0[:, 3:4], None, ALU.mult).then_inc(v_c2, 1)
            v.wait_ge(pe_c2, 1)
            nc.vector.tensor_tensor(W0_bc[:], O[:, 0:C], b2_bc[:], ALU.add)
            nc.vector.drain().then_inc(v_setup, 1)

            def main_product(t, g):
                rr = (t_ring[0] - 2) % RING
                v.wait_ge(w_mm[g], t - 1)
                wait(v, scat_mm[g], t - 2)
                y = Y[:, rr, :, :]
                if g == 0:
                    y = Y[:, rr, 0, :].unsqueeze(1).broadcast_to([N, PER, C])
                if g == 2:
                    y = Y[:, rr, 2, :].unsqueeze(1).broadcast_to([N, PER, C])
                nc.vector.tensor_tensor(P[:, g, :].rearrange("p (t c) -> p t c", t=PER),
                                        Wb[:].rearrange("p (t c) -> p t c", t=PER), y, ALU.mult).then_inc(p_ready[g], 1)

            def one_hots(t, g):
                rr = (t_ring[0] - 2) % RING
                v.wait_ge(s["rc_ready"], t - 1)
                wait(v, scat_mm[g], t - 2)
                for q in range(PER * g, PER * g + PER):
                    last = one_hot(q, SV[:, rr, 1, q:q + 1], RC[:, rr, q:q + 1])
                last.then_inc(oh_ready[g], 1)

            t_ring = [0]

            def step(t, cyc, r):
                t_ring[0] = r
                tab = TAB[:, r, :, :]
                adj = pair(ADJ[:, r, :])
                if on(t, "A"):
                    v.wait_ge(loadA[r], cyc * 32 + 32)
                    nc.vector.scalar_tensor_tensor(KEY[:], adj, CUTOFF, adj, ALU.is_lt, ALU.mult).then_inc(s["key_ready"], 1)
                    wait(v, s["agg_mm"], t - 2)
                    nc.vector.tensor_scalar(M0[:, r, :], ADJ[:, r, :], 0.0, None, ALU.is_equal).then_inc(s["m0_ready"], 1)
                    nc.vector.drain()
                    for g in range(G):
                        nc.vector.max(tab[:, g, 0:8], KEY[:, g, :])
                if on(t, "B2"):
                    one_hots(t, 0)
                if on(t, "A"):
                    nc.vector.drain()
                    for g in range(G):
                        nc.vector.match_replace(KEY2[:, g, :], tab[:, g, 0:8], KEY[:, g, :], -1.0)
                        nc.vector.max_index(IDX[:, g, 0:8], tab[:, g, 0:8], KEY[:, g, :])
                    nc.vector.drain()
                    for g in range(G):
                        nc.vector.max(tab[:, g, 8:16], KEY2[:, g, :])
                    nc.vector.drain()
                    nc.vector.tensor_scalar(over[:], tab[:, :, MAIN:16], 0.0, None, ALU.is_gt)
                    for g in range(G):
                        nc.vector.max_index(IDX[:, g, 8:16], tab[:, g, 8:16], KEY2[:, g, :])
                    nc.vector.drain()
                    nc.vector.tensor_reduce(cnt[:, r, :], over[:], AX.X, ALU.add).then_inc(s["cnt_ready"], 1)
                    nc.vector.tensor_copy(tab[:, :, 16:32], IDX[:])
                if on(t, "B2"):
                    main_product(t, 0)
                if on(t, "C1"):
                    v_c1_min(v, s, t - 3)
                if on(t, "B2"):
                    one_hots(t, 1)
                if on(t, "A"):
                    v.wait_ge(s["rank_mm"], t + 1)
                    nc.vector.tensor_copy(tab[:, :, 32], RANK)
                    nc.vector.tensor_copy(news[:, 1:3], tab[:, :, 15])
                    nc.vector.drain()
                    nc.vector.tensor_tensor(end[:], tab[:, :, 32], cnt[:, r, :], ALU.add)
                    for g in range(G):
                        nc.vector.tensor_scalar(SELa[:, g, :], iota[:], tab[:, g, 32:33], None, ALU.is_ge)
                    nc.vector.drain()
                    wait(v, s["gather_mm"], t)
                    for g in range(G):
                        last = nc.vector.scalar_tensor_tensor(SEL[:, g, :], iota[:], end[:, g:g + 1], SELa[:, g, :],
                                                              ALU.is_lt, ALU.mult)
                    last.then_inc(s["sel_ready"], 1)
                if on(t, "C1"):
                    v_c1_max(v, s, t - 3)
                if on(t, "B2"):
                    main_product(t, 1)
                if on(t, "A"):
                    nc.vector.tensor_scalar(news[:, 3:5], end[:], float(N), None, ALU.subtract)
                    nc.vector.drain()
                    v.wait_ge(s["neg_ready"], t + 1)
                    nc.vector.tensor_tensor(flags[:, 0:5], flags[:, 0:5], news[:, 0:5], ALU.max).then_inc(s["rank_read"], 1)
                if on(t, "B2"):
                    one_hots(t, 2)
                if on(t, "C1"):
                    v_c1_residual(v, s, t - 3, turn(cyc, r, 3)[1])
                if on(t, "A"):
                    v.wait_ge(s["ovt_ready"], t + 1)
                    nc.vector.tensor_scalar(rel[:], OVT[:, :, 32], part5[:, 0:1], -1.0, ALU.subtract, ALU.mult)
                    for g, q in ((0, 0), (1, 8)):
                        nc.vector.tensor_copy(SV[:, r, :, q:q + 4],
                                              tab[:, g, 0:32].rearrange("p (k c) -> p k c", k=2)[:, :, 0:4])
                    nc.vector.tensor_copy(SV[:, r, :, 4:8:2],
                                          tab[:, :, 0:32].rearrange("p g (k c) -> p k g c", k=2)[:, :, :, 4])
                    nc.vector.drain()
                    nc.vector.tensor_tensor(mask[:], iota[:, 0:16].unsqueeze(1).broadcast_to([N, G, 16]),
                                            rel[:].unsqueeze(2).broadcast_to([N, G, 16]), ALU.is_equal)
                    nc.vector.drain()
                    nc.vector.tensor_tensor(picked[:], OVT[:, :, 0:32].rearrange("p g (k c) -> p g k c", k=2),
                                            mask[:].unsqueeze(2).broadcast_to([N, G, 2, 16]), ALU.mult)
                    nc.vector.drain()
                    nc.vector.tensor_reduce(SV[:, r, :, 5:8:2].rearrange("p k g -> p g k"), picked[:],
                                            AX.X, ALU.add).then_inc(s["slots_ready"], 1)
                    nc.vector.drain()
                    wait(v, s["bcast_mm"], t)
                    nc.vector.tensor_copy(VB[:], SV[:, r, 0, :].unsqueeze(2).broadcast_to([N, SLOTS, 32])).then_inc(s["vb_ready"], 1)
                if on(t, "B2"):
                    main_product(t, 2)
                if on(t, "C1"):
                    v_norm(v, s["rs1_ready"], s["x1_ready"], t - 3, 0, Z, X1[:, turn(cyc, r, 3)[1], :])
                if on(t, "C2"):
                    v_c2_act(v, s, t - 4)
                    v.wait_ge(s["z2_ready"], t - 3)
                    v_stats(Z2, 1, s["mv2_ready"])
                    rr = turn(cyc, r, 4)[1]
                    if not isinstance(t, int) or t - 4 >= RING:
                        v.wait_ge(stored[rr], turn(cyc, r, 4)[0] * 16)
                    v_norm(v, s["rs2_ready"], s["out_ready"], t - 4, 1, Z2, OUT[:, rr, :])

            steps(v, step)

            nc.vector.drain()
            nc.vector.tensor_reduce(flag1[:], flags[:], AX.X, ALU.max)
            nc.vector.drain()
            nc.vector.tensor_scalar(flag2[:], flag1[:], 0.0, None, ALU.is_gt).then_inc(flag_v, 1)
            v.wait_ge(flag_pe, 1)
            nc.vector.tensor_scalar(flag_i[:], M[0:1, 0:1], 0.0, None, ALU.is_gt).then_inc(flag_ready, 1)
            v.wait_ge(flag_ready, 1)
            general = v.value_load(flag_i[0:1, 0:1], min_val=0, max_val=1)
            with v.If(general > 0):
                with v.Fori(0, PAIRS) as n:
                    v.wait_ge(g_load, n * 64 + 64)
                    nc.vector.tensor_scalar(g_k[:], ADJ[:, 0, :], 0.1, MAGIC, ALU.mult, ALU.add)
                    nc.vector.drain()
                    nc.vector.tensor_scalar(g_k[:], g_k[:], MAGIC, None, ALU.subtract)
                    nc.vector.drain()
                    nc.vector.scalar_tensor_tensor(g_u[:], g_k[:], -10.0, ADJ[:, 0, :], ALU.mult, ALU.add)
                    nc.vector.drain()
                    nc.vector.tensor_tensor(g_u[:], g_u[:], g_u[:], ALU.mult)
                    nc.vector.drain()
                    nc.vector.tensor_scalar(g_k[:], g_u[:], COS[7], None, ALU.mult)
                    for k in range(6, 0, -1):
                        nc.vector.drain()
                        nc.vector.scalar_tensor_tensor(g_k[:], g_k[:], COS[k], g_u[:], ALU.add, ALU.mult)
                    nc.vector.drain()
                    nc.vector.tensor_scalar(g_k[:], g_k[:], COS[0], None, ALU.add)
                    nc.vector.drain()
                    nc.vector.tensor_tensor(g_k[:], g_k[:], g_k[:], ALU.mult)
                    nc.vector.drain()
                    nc.vector.scalar_tensor_tensor(g_rc[:], ADJ[:, 0, :], CUTOFF, g_k[:], ALU.is_lt, ALU.mult)
                    nc.vector.memset(AGG[:], 0.0)
                    nc.vector.tensor_tensor(pair(XB[:, 0, :]), pair(X[:, 0, :]),
                                            ob2_bc[:].unsqueeze(1).broadcast_to([N, G, C]), ALU.add).then_inc(gs["xb_ready"], 1)
                    nc.vector.drain()
                    for g in range(G):
                        with v.Fori(0, N // PER) as i:
                            m = n * (G * N // PER) + i + g * (N // PER)
                            nc.vector.tensor_copy(g_val[:], ADJ[:, 0, bass.ds(i * PER + g * N, PER)])
                            nc.vector.tensor_copy(g_w[:], g_rc[:, bass.ds(i * PER + g * N, PER)])
                            nc.vector.tensor_copy(g_idx[:], iota[:, bass.ds(i * PER, PER)])
                            nc.vector.drain()
                            nc.vector.tensor_copy(g_vb[:], g_val[:].unsqueeze(2).broadcast_to([N, PER, 32])).then_inc(gs["pick"], 1)
                            for q in range(PER):
                                one_hot(q, g_idx[:, q:q + 1], g_w[:, q:q + 1])
                            v.wait_ge(gs["h_mm"], m + 1)
                            nc.vector.tensor_scalar(E[:, :, 0:N], H[:, :, 0:N], FB1, CLAMP, ALU.add, ALU.min).then_inc(gs["hm"], 1)
                            v.wait_ge(gs["l"], m + 1)
                            nc.vector.scalar_tensor_tensor(S[:, 0, :, 0:N], H[:, :, 0:N], FB1L, E[:, :, 0:N],
                                                           ALU.add, ALU.max).then_inc(gs["s"], 1)
                            v.wait_ge(gs["y_ready"], n * 2 + (g + 1))
                            v.wait_ge(gs["w_mm"], m + 1)
                            nc.vector.tensor_tensor(P[:, 0, :].rearrange("p (t c) -> p t c", t=PER),
                                                    Wb[:].rearrange("p (t c) -> p t c", t=PER),
                                                    Y[:, 0, 0, :].unsqueeze(1).broadcast_to([N, PER, C]), ALU.mult)
                            nc.vector.drain().then_inc(gs["p"], 1)
                            v.wait_ge(gs["scat"], m + 1)
                            nc.vector.tensor_tensor(AGG[:, g * N:(g + 1) * N], AG[:, 0:N], AGG[:, g * N:(g + 1) * N], ALU.add)
                            nc.vector.drain()
                    nc.vector.drain().then_inc(gs["agg"], 1)
                    v_c1_min(v, gs, n)
                    v_c1_max(v, gs, n)
                    v_c1_residual(v, gs, n, 0)
                    v_norm(v, gs["rs1_ready"], gs["x1_ready"], n, 0, Z, X1[:, 0, :])
                    v_c2_act(v, gs, n)
                    nc.vector.drain()
                    nc.vector.tensor_tensor(Z2[:], V[:], X1[:, 0, :], ALU.add)
                    nc.vector.drain()
                    v_stats(Z2, 1, gs["mv2_ready"])
                    v_norm(v, gs["rs2_ready"], gs["out_ready"], n, 1, Z2, OUT[:, 0, :])
                v.nop()

        def mm(o, w, m, start=True, stop=True):
            return nc.tensor.matmul(o, w, m, start=start, stop=stop)

        def pe_ow1(pe, q, n):
            for g in range(G):
                last = mm(T1[:, g, :], ow1s[:], AGG[:, g * N:(g + 1) * N])
            last.then_inc(q["ow1_mm"], 1)

        def pe_ow2(pe, q, n):
            pe.wait_ge(q["s2_ready"], n + 1)
            for g in range(G):
                last = mm(T2[:, g, :], S2[:, g * N:(g + 1) * N], ow2s[:])
            last.then_inc(q["ow2_mm"], 1)

        def pe_agg2(pe, q, n, rr):
            pe.wait_ge(q["x1_ready"], n + 1)
            for g in range(G):
                last = mm(T3[:, g, :], X1[:, rr, g * C:(g + 1) * C], ADJ2[:, rr, g * N:(g + 1) * N])
            last.then_inc(q["a2_mm"], 1)
            for g in range(G):
                last = mm(NS[:, g:g + 1], ADJ2[:, rr, g * N:(g + 1) * N], ones[:, 0:1])
            last.then_inc(q["ns_mm"], 1)

        def pe_out(pe, q, n):
            pe.wait_ge(q["a2_ready"], n + 1)
            for g in range(G):
                last = mm(T4[:, g, :], A2[:, g * N:(g + 1) * N], WTs[:])
            last.then_inc(q["out_mm"], 1)

        def filter_out(rr, g, src):
            mm(Wb[:], ones_h[:], b2_rows[:].rearrange("p t c -> p (t c)"), stop=False)
            for t in range(PER):
                last = mm(Wb[:, t * C:(t + 1) * C], src[:, rr, t, g * N:(g + 1) * N], fw2s[:], start=False, stop=(t == PER - 1))
            return last

        @block.tensor
        def _(pe):
            pe.wait_ge(a_c1, 1)
            mm(M[:, 0:1], fw1s[0:R, :], f0[0:R, 1:2]).then_inc(pe_c1, 1)
            pe.wait_ge(v_c2, 2)
            mm(O[:, 0:C], S2[:, 0:N], fw2s[:]).then_inc(pe_c2, 1)
            pe.wait_ge(v_setup, 1)

            def w_group(t, rr, g):
                pe.wait_ge(s["s_ready"], t - 1)
                if g:
                    pe.wait_ge(p_ready[g - 1], t - 1)
                else:
                    wait(pe, p_ready[GROUPS - 1], t - 2)
                filter_out(rr, g, S).then_inc(w_mm[g], 1)

            def scatter(t, rr, g):
                pe.wait_ge(p_ready[g], t - 1)
                pe.wait_ge(oh_ready[g], t - 1)
                for i in range(PER):
                    q = PER * g + i
                    h = GRAPH_OF[q]
                    if q == MAIN + 1:
                        zeros(t, rr, 0)
                    last = mm(AG[:, h * N:(h + 1) * N], P[:, g, i * C:(i + 1) * C], OH[:, q, :],
                              start=(q in (0, MAIN + 1)), stop=False)
                last.then_inc(scat_mm[g], 1)

            def zeros(t, rr, h):
                return mm(AG[:, h * N:(h + 1) * N], YW0[:, rr, h, :], M0[:, rr, h * N:(h + 1) * N], start=False)

            def step(t, cyc, r):
                r1, r2, r4 = turn(cyc, r, 1)[1], turn(cyc, r, 2)[1], turn(cyc, r, 4)[1]
                wait(pe, s["z_ready"], min(t - 3, PAIRS) if isinstance(t, int) else t - 3)
                wait(pe, s["u_ready"], t - 4)
                if on(t, "B1"):
                    pe.wait_ge(s["f_ready"], t)
                    for i in range(PER):
                        last = mm(H[:, i, 0:GROUPS * N], fw1s[32 * i:32 * i + R, :], FT[32 * i:32 * i + R, r1, :])
                    last.then_inc(s["h_mm"], 1)
                if on(t, "A"):
                    pe.wait_ge(loadA[r], cyc * 32 + 32)
                    wait(pe, s["sq_ready"], t)
                    for g in range(G):
                        last = mm(M[:, g * C:(g + 1) * C], XT[:, r, g * N:(g + 1) * N], win[:])
                    last.then_inc(s["y_mm"], 1)
                if on(t, "B2"):
                    w_group(t, r2, 0)
                if on(t, "B1"):
                    pe.wait_ge(s["e_ready"], t)
                if on(t, "C1"):
                    pe.wait_ge(s["agg_ready"], t - 2)
                    pe_ow1(pe, s, t - 3)
                if on(t, "C2"):
                    pe.wait_ge(loadD[r4], turn(cyc, r, 4)[0] * 16 + 16)
                    pe_agg2(pe, s, t - 4, r4)
                if on(t, "A"):
                    pe.wait_ge(s["cnt_ready"], t + 1)
                    pe.wait_ge(s["y_ready"], t + 1)
                    mm(RANK, upper[:], cnt[:, r, :]).then_inc(s["rank_mm"], 1)
                if on(t, "B2"):
                    w_group(t, r2, 1)
                if on(t, "B2"):
                    wait(pe, s["agg_ready"], t - 2)
                    scatter(t, r2, 0)
                if on(t, "C1"):
                    pe_ow2(pe, s, t - 3)
                if on(t, "A"):
                    pe.wait_ge(s["sel_ready"], t + 1)
                    wait(pe, s["yo_ready"], t)
                    for g in range(G):
                        mm(GY[:, g * C:(g + 1) * C], SEL[:, g, :], Y[:, r, 2 * g, :])
                        last = mm(GT[:, g, :], SEL[:, g, :], TAB[:, r, g, :])
                    last.then_inc(s["gather_mm"], 1)
                if on(t, "B2"):
                    w_group(t, r2, 2)
                if on(t, "C2"):
                    pe_out(pe, s, t - 4)
                if on(t, "A"):
                    pe.wait_ge(s["vb_ready"], t + 1)
                    for g in range(GROUPS):
                        src = VB[:, PER * g:PER * g + PER, :].rearrange("p t r -> p (t r)")
                        last = nc.tensor.transpose(M[:, g * N:(g + 1) * N], src, ident[:])
                    last.then_inc(s["bcast_mm"], 1)
                if on(t, "B2"):
                    pe.wait_ge(s["yw0_ready"], t - 1)
                    pe.wait_ge(s["m0_ready"], t - 1)
                    scatter(t, r2, 1)
                    scatter(t, r2, 2)
                    zeros(t, r2, 1).then_inc(s["agg_mm"], 1)

            steps(pe, step)

            pe.wait_ge(flag_v, 1)
            mm(M[0:1, 0:1], flag2[:], ones[:, 0:1]).then_inc(flag_pe, 1)
            pe.wait_ge(flag_ready, 1)
            general = pe.value_load(flag_i[0:1, 0:1], min_val=0, max_val=1)
            with pe.If(general > 0):
                with pe.Fori(0, PAIRS) as n:
                    pe.wait_ge(g_load, n * 64 + 64)
                    for g in range(G):
                        mm(M[:, 0:C], XT[:, 0, g * N:(g + 1) * N], win[:]).then_inc(gs["y_mm"], 1)
                        with pe.Fori(0, N // PER) as i:
                            m = n * (G * N // PER) + i + g * (N // PER)
                            pe.wait_ge(gs["pick"], m + 1)
                            pe.wait_ge(gs["y_ready"], n * 2 + (g + 1))
                            nc.tensor.transpose(M[:, 0:N], g_vb[:].rearrange("p t r -> p (t r)"), ident[:]).then_inc(gs["bcast"], 1)
                            pe.wait_ge(gs["f"], m + 1)
                            for k in range(PER):
                                last = mm(H[:, k, 0:N], fw1s[32 * k:32 * k + R, :], FT[32 * k:32 * k + R, 0, 0:N])
                            last.then_inc(gs["h_mm"], 1)
                            pe.wait_ge(gs["s"], m + 1)
                            filter_out(0, 0, S).then_inc(gs["w_mm"], 1)
                            pe.wait_ge(gs["p"], m + 1)
                            for k in range(PER):
                                last = mm(AG[:, 0:N], P[:, 0, k * C:(k + 1) * C], OH[:, k, :], start=(k == 0), stop=(k == PER - 1))
                            last.then_inc(gs["scat"], 1)
                    pe.wait_ge(gs["agg"], n + 1)
                    pe_ow1(pe, gs, n)
                    pe_ow2(pe, gs, n)
                    pe_agg2(pe, gs, n, 0)
                    pe_out(pe, gs, n)
                pe.nop()


def kernel(**inputs):
    import numpy as _np
    import concourse.bacc as _bacc
    from concourse import mybir as _mybir
    from concourse.bass_utils import run_bass_kernel_spmd as _run

    def pairs(a):
        return a.reshape(PAIRS, G, N, N).transpose(0, 2, 1, 3).reshape(PAIRS, N, G * N)

    def col(a):
        return a.reshape(-1, 1)

    given = {k: _np.asarray(v) for k, v in inputs.items()}
    x, adj, fw1 = given["x"], given["adj"], given["L0_gnn_fw1"]
    layouts = {
        "x": pairs(x),
        "xT": pairs(x.transpose(0, 2, 1)),
        "adjT": pairs(adj.transpose(0, 2, 1)),
        "widths": col(given["L0_gnn_widths"]),
        "offsets": col(given["L0_gnn_offsets"]),
        "w_in2f": given["L0_gnn_w_in2f"],
        "fw1": fw1,
        "fw1T": fw1.T,
        "fb1": col(given["L0_gnn_fb1"]),
        "fw2": given["L0_gnn_fw2"],
        "fb2": given["L0_gnn_fb2"],
        "ow1": given["L0_gnn_ow1"],
        "ob1": col(given["L0_gnn_ob1"]),
        "ow2": given["L0_gnn_ow2"],
        "ob2": given["L0_gnn_ob2"],
        "WT": given["L1_gnn_W"].T,
        "bL": given["L1_gnn_b"],
    }
    nc = _bacc.Bacc("TRN2", target_bir_lowering=False, num_devices=1)
    arrays, args = {}, []
    for name, a in layouts.items():
        a = _np.ascontiguousarray(a)
        arrays[f"in_{name}"] = a
        args.append(nc.dram_tensor(f"in_{name}", a.shape, _mybir.dt.from_np(a.dtype), kind="ExternalInput").ap())
    args.append(nc.dram_tensor("result", (PAIRS, N, G * C), _mybir.dt.float32, kind="ExternalOutput").ap())
    build(nc, *args)
    r = _run(nc, [arrays], core_ids=[0])
    got = r.results[0]["result"]
    return _np.ascontiguousarray(got.reshape(PAIRS, N, G, C).transpose(0, 2, 1, 3).reshape(B, N, C))
```

```python
import math
from contextlib import ExitStack

import concourse.bass as bass
from concourse import mybir

F32 = mybir.dt.float32
BF16 = mybir.dt.bfloat16
U32 = mybir.dt.uint32
I32 = mybir.dt.int32
ALU = mybir.AluOpType
ACT = mybir.ActivationFunctionType
AX = mybir.AxisListType

B, N, C, R = 64, 128, 128, 20
PAIRS = B // 2
G = 2
TAB = 34
MAIN = 5
SLOTS = G * (MAIN + 1)
GROUPS, PER = SLOTS // 4, 4
RING = 3
PACKED = 6 * C + 4 + R
CUTOFF = 5.0
LN2 = math.log(2.0)
CLAMP = 40.0
EPS = 1e-5
MAGIC = 1.5 * 2.0 ** 23
COS = [(-1.0) ** k * (math.pi / 10) ** (2 * k) / math.factorial(2 * k) for k in range(7)]
GRAPH_OF = [0, 0, 0, 0, 0, 0, 1, 1, 1, 1, 1, 1]


def build(nc, x, xT, adjT, weights, biases, out):
    ctx = ExitStack()
    with ctx:
        def sb(name, shape, dt=F32):
            return ctx.enter_context(nc.sbuf_tensor(name, shape, dt))

        def pb(name, shape):
            return ctx.enter_context(nc.psum_tensor(name, shape, F32))

        def sem(name):
            return ctx.enter_context(nc.semaphore(name))

        iota_i = sb("iota_i", [N, N], I32)
        part_i = sb("part_i", [N, 1], I32)
        iota = sb("iota", [N, N])
        part = sb("part", [N, 1])
        part5 = sb("part5", [N, 1])
        ident = sb("ident", [N, N])
        upper = sb("upper", [N, N])
        ones = sb("ones", [N, N])
        ones_h = sb("ones_h", [N, N], BF16)
        packed = sb("packed", [N, PACKED])
        win, fw2s, ow1s, ow2s, WTs = (packed[:, k * C:(k + 1) * C] for k in range(5))
        fw1s = packed[:, 5 * C:6 * C]
        FB1, OB1, width_c, noff_c = (packed[:, 6 * C + k:6 * C + k + 1] for k in range(4))
        fw1T = packed[:, 6 * C + 4:6 * C + 4 + R]
        cols = sb("cols", [C, 4])
        FB1L, OB1L, EPSC, coef_c = (cols[:, k:k + 1] for k in range(4))
        rows = sb("rows", [N, 3 * C])
        b2_bc, ob2_bc, bL_bc = (rows[:, k * C:(k + 1) * C] for k in range(3))
        b2_hi = sb("b2_hi", [N, C], BF16)
        b2_mid = sb("b2_mid", [N, C], BF16)
        b2_res = sb("b2_res", [N, C])
        b2_sel = sb("b2_sel", [N, C])
        b2_rows = sb("b2_rows", [N, PER, C], BF16)
        W0_bc = sb("W0_bc", [N, C])
        f0 = sb("f0", [N, 2])
        s0 = sb("s0", [C, 4])
        hsum = sb("hsum", [C, R + 1])

        ADJ = sb("ADJ", [N, RING, G * N])
        XT = sb("XT", [C, RING, G * N])
        KEY = sb("KEY", [N, G, N])
        KEY2 = sb("KEY2", [N, G, N])
        IDX = sb("IDX", [N, G, 16], U32)
        over = sb("over", [N, G, 16 - MAIN])
        cnt = sb("cnt", [N, RING, G])
        end = sb("end", [N, G])
        SEL = sb("SEL", [N, G, N])
        SELa = sb("SELa", [N, G, N])
        rel = sb("rel", [N, G])
        mask = sb("mask", [N, G, 16])
        picked = sb("picked", [N, G, 2, 16])
        SV = sb("SV", [N, RING, 2, SLOTS])
        RC = sb("RC", [N, RING, SLOTS])
        VB = sb("VB", [N, SLOTS, 32])
        usq = sb("usq", [N, SLOTS])
        acc = sb("acc", [N, SLOTS])
        live = sb("live", [N, SLOTS])
        YT = sb("YT", [N, RING, 2 * G, C + TAB])
        M0 = sb("M0", [N, RING, G * N])
        YW0 = sb("YW0", [N, RING, G, C])
        SQ = sb("SQ", [N, GROUPS * N])
        FT = sb("FT", [N, RING, GROUPS * N])
        negs = sb("negs", [N, G * N])
        news = sb("news", [N, 8])
        flags = sb("flags", [N, 8])
        E = sb("E", [C, PER, GROUPS * N])
        S = sb("S", [C, RING, PER, GROUPS * N])
        P = sb("P", [N, GROUPS, PER * C])
        OH = sb("OH", [N, SLOTS, N])
        AGG = sb("AGG", [C, G * N])
        X = sb("X", [N, RING, G * C])
        XB = sb("XB", [N, RING, G * C])
        HM = sb("HM", [C, G * N])
        L2 = sb("L2", [C, G * N])
        S2 = sb("S2", [C, G * N])
        Z = sb("Z", [N, G * C])
        st = sb("st", [N, 2, G, 6])
        mv = sb("mv", [N, 2, G, 2])
        lnv = sb("lnv", [N, 2, G])
        rstd = sb("rstd", [N, 2, G])
        shift = sb("shift", [N, 2, G])
        X1 = sb("X1", [N, RING, G * C])
        ADJ2 = sb("ADJ2", [N, RING, G * N])
        A2 = sb("A2", [C, G * N])
        rn = sb("rn", [N, G])
        U = sb("U", [N, G * C])
        V = sb("V", [N, G * C])
        Z2 = sb("Z2", [N, G * C])
        OUT = sb("OUT", [N, RING, G * C])
        g_rc = sb("g_rc", [N, G * N])
        g_k = sb("g_k", [N, G * N])
        g_u = sb("g_u", [N, G * N])
        g_val = sb("g_val", [N, PER])
        g_vb = sb("g_vb", [N, PER, 32])
        g_idx = sb("g_idx", [N, PER])
        g_w = sb("g_w", [N, PER])
        flag1 = sb("flag1", [N, 1])
        flag2 = sb("flag2", [N, 1])
        flag_i = sb("flag_i", [1, 1], I32)

        H = pb("H", [N, PER, 512])
        Wb = pb("Wb", [N, PER * C])
        AG = pb("AG", [N, 512])
        M = pb("M", [N, 512])
        O = pb("O", [N, 512])
        HH = H[:, :, 0:GROUPS * N]
        T1, T2, T3, T4 = (H[:, k, 0:G * N].rearrange("p (g c) -> p g c", g=G) for k in range(4))
        RANK = M[:, 504:506]
        GO = O[:, 0:G * (C + TAB)].rearrange("p (g c) -> p g c", g=G)
        NS = H[:, 3, G * C:G * C + G]

        def pair(t):
            return t.rearrange("p (g c) -> p g c", g=G)

        c_dma = sem("c_dma")
        pool_consts = sem("pool_consts")
        v_consts = sem("v_consts")
        v_c1 = sem("v_c1")
        v_c2 = sem("v_c2")
        a_c1 = sem("a_c1")
        a_c2 = sem("a_c2")
        pe_c1 = sem("pe_c1")
        pe_c2 = sem("pe_c2")
        v_setup = sem("v_setup")
        loadA = [sem(f"loadA{r}") for r in range(RING)]
        loadX = [sem(f"loadX{r}") for r in range(RING)]
        loadD = [sem(f"loadD{r}") for r in range(RING)]
        stored = [sem(f"stored{r}") for r in range(RING)]
        names = ("key_ready top8_ready key2_ready top16_ready over_ready idx_ready cnt_ready news_ready rank_mm rank_ready sela_ready sel_ready "
                 "y_mm y_ready gather_mm yo_ready rel_ready mask_ready picked_ready slots_ready vb_ready "
                 "m0_ready yw0_ready rc_ready bcast_mm sq_ready f_ready neg_ready h_mm e_ready s_ready "
                 "agg_mm agg_ready ow1_mm e2_ready s2_ready ow2_mm xb_ready z_ready "
                 "x1_ready a2_mm ns_mm a2_ready out_mm rn_ready u_ready v_ready z2_ready out_ready "
                 "flags_ready st_ready mv_ready rs_ready shift_ready").split()
        s = {k: sem(k) for k in names}
        w_mm = [sem(f"w_mm{g}") for g in range(GROUPS)]
        p_ready = [sem(f"p_ready{g}") for g in range(GROUPS)]
        oh_ready = [sem(f"oh_ready{g}") for g in range(GROUPS)]
        scat_mm = [sem(f"scat_mm{g}") for g in range(GROUPS)]
        oh_pool = sem("oh_pool")
        own = sem("own")
        flag_v = sem("flag_v")
        flag_pe = sem("flag_pe")
        flag_ready = sem("flag_ready")
        g_load = sem("g_load")
        g_stored = sem("g_stored")
        g_pair_done = sem("g_pair_done")
        gnames = ("rc y_mm y_ready pick bcast f h_mm hm l s w_mm p scat add agg "
                  "ow1_mm hm_ready l2_ready s2_ready ow2_mm z_ready xb_ready "
                  "x1_ready a2_mm ns_mm a2_ready out_mm rn_ready u_ready v_ready out_ready mv_ready rs_ready shift_ready").split()
        gs = {k: sem("g_" + k) for k in gnames}

        def wait(eng, which, value):
            if not isinstance(value, int) or value > 0:
                eng.wait_ge(which, value)

        block = ctx.enter_context(nc.Block())

        LAG = {"A": 0, "B1": 1, "B2": 2, "C1": 3, "N1": 4, "C2": 4, "N2": 5}
        AHEAD = 2

        def steps(eng, step, lag=LAG["N2"]):
            first = lag + 1
            rolls = (PAIRS - first) // RING
            for t in range(first):
                step(t, t // RING, t % RING)
            with eng.Fori(0, rolls) as q:
                for k in range(RING):
                    c = first + k
                    step(q * RING + c, q + c // RING, c % RING)
            for t in range(first + RING * rolls, PAIRS + lag):
                step(t, t // RING, t % RING)

        def on(t, stage):
            return not isinstance(t, int) or 0 <= t - LAG[stage] < PAIRS

        def turn(cyc, r, lag):
            return cyc + (r - lag) // RING, (r - lag) % RING

        def load_a(sp, n, r):
            wait(sp, s["key_ready"], n - 2)
            wait(sp, s["y_mm"], n - 2)
            wait(sp, s["m0_ready"], n - 2)
            wait(sp, s["neg_ready"], n - 2)
            sp.dma_start(ADJ[:, r, :], adjT[n]).then_inc(loadA[r], 16)
            sp.dma_start(XT[:, r, :], xT[n]).then_inc(loadA[r], 16)

        def load_x(sp, n, r):
            wait(sp, s["xb_ready"], n - 2)
            sp.dma_start(X[:, r, :], x[n]).then_inc(loadX[r], 16)

        def load_d(sp, n, r):
            wait(sp, s["ns_mm"], n - 2)
            sp.dma_start(ADJ2[:, r, :], adjT[n]).then_inc(loadD[r], 16)

        @block.sync
        def _(sp):
            sp.dma_start(ADJ[:, 0, :], adjT[0]).then_inc(loadA[0], 16)
            sp.dma_start(packed[:], weights).then_inc(c_dma, 16)
            sp.dma_start(XT[:, 0, :], xT[0]).then_inc(loadA[0], 16)
            sp.dma_start(rows[:], biases.partition_broadcast(N)).then_inc(c_dma, 16)

            def step(t, cyc, r):
                def has(lag):
                    return not isinstance(t, int) or 0 <= t - lag < PAIRS

                if has(0) and not (isinstance(t, int) and t == 0):
                    load_a(sp, t, r)
                if has(LAG["C1"]):
                    load_x(sp, t - LAG["C1"], turn(cyc, r, LAG["C1"])[1])
                if has(LAG["C2"]):
                    load_d(sp, t - LAG["C2"], turn(cyc, r, LAG["C2"])[1])
                lag = LAG["N2"] + AHEAD
                if has(lag):
                    rr = turn(cyc, r, lag)[1]
                    wait(sp, s["out_ready"], t - lag + 1)
                    sp.dma_start(out[t - lag], OUT[:, rr, :]).then_inc(stored[rr], 16)

            steps(sp, step, LAG["N2"] + AHEAD)
            for r in range(RING):
                sp.wait_ge(stored[r], 16 * ((PAIRS - r + RING - 1) // RING))
            sp.wait_ge(flag_ready, 1)
            general = sp.value_load(flag_i[0:1, 0:1], min_val=0, max_val=1)
            with sp.If(general > 0):
                with sp.Fori(0, PAIRS) as n:
                    sp.dma_start(ADJ[:, 0, :], adjT[n]).then_inc(g_load, 16)
                    sp.dma_start(ADJ2[:, 0, :], adjT[n]).then_inc(g_load, 16)
                    sp.dma_start(XT[:, 0, :], xT[n]).then_inc(g_load, 16)
                    sp.dma_start(X[:, 0, :], x[n]).then_inc(g_load, 16)
                    sp.wait_ge(gs["out_ready"], n + 1)
                    sp.dma_start(out[n], OUT[:, 0, :]).then_inc(g_stored, 16)
                    sp.wait_ge(g_stored, n * 16 + 16)
                    sp.sem_inc(g_pair_done, 1)
                sp.nop()

        POOL_HOT = range(8, 12)

        def one_hot(eng, q, idx, w):
            return eng.tensor_scalar(OH[:, q, :], iota[:], idx, w, ALU.is_equal, ALU.mult)

        @block.gpsimd
        def _(pool):
            nc.gpsimd.iota(iota_i[:], pattern=[[1, N]], base=0, channel_multiplier=0).then_inc(pool_consts, 1)
            nc.gpsimd.iota(part_i[:], pattern=[[1, 1]], base=0, channel_multiplier=1).then_inc(pool_consts, 1)
            pool.wait_ge(c_dma, 32)

            def step(t, cyc, r):
                if on(t, "B2"):
                    wait(pool, scat_mm[2], t - 2)
                if on(t, "C1"):
                    c, rr = turn(cyc, r, 3)
                    wait(pool, loadX[rr], c * 16 + 16)
                    nc.gpsimd.tensor_tensor(pair(XB[:, rr, :]), pair(X[:, rr, :]),
                                            ob2_bc.unsqueeze(1).broadcast_to([N, G, C]), ALU.add).then_inc(s["xb_ready"], 1)
                if on(t, "B2"):
                    rr = turn(cyc, r, 2)[1]
                    for q in POOL_HOT:
                        last = one_hot(nc.gpsimd, q, SV[:, rr, 1, q:q + 1], RC[:, rr, q:q + 1])
                    last.then_inc(oh_pool, 1)
                if on(t, "A"):
                    if isinstance(t, int) and t == 0:
                        pool.wait_ge(v_setup, 1)
                    wait(pool, s["agg_mm"], t - 2)
                    wait(pool, s["y_ready"], t + 1)
                    nc.gpsimd.tensor_tensor(YW0[:, r, :, :], YT[:, r, 0:2 * G:2, 0:C],
                                            W0_bc[:].unsqueeze(1).broadcast_to([N, G, C]), ALU.mult).then_inc(s["yw0_ready"], 1)
                if on(t, "C2"):
                    rr = turn(cyc, r, 4)[1]
                    wait(pool, s["v_ready"], t - 3)
                    wait(pool, s["out_ready"], t - 4)
                    nc.gpsimd.tensor_tensor(Z2[:], V[:], X1[:, rr, :], ALU.add).then_inc(s["z2_ready"], 1)
                if on(t, "A"):
                    wait(pool, s["slots_ready"], t + 1)
                    val = SV[:, r, 0, :]
                    nc.gpsimd.tensor_tensor(usq[:], val, val, ALU.mult)
                    nc.gpsimd.tensor_scalar(live[:], val, 0.0, None, ALU.is_gt)
                    nc.gpsimd.drain()
                    nc.gpsimd.tensor_scalar(acc[:], usq[:], COS[6], COS[5], ALU.mult, ALU.add)
                    for k in range(4, -1, -1):
                        nc.gpsimd.drain()
                        nc.gpsimd.tensor_tensor(acc[:], acc[:], usq[:], ALU.mult)
                        nc.gpsimd.drain()
                        nc.gpsimd.tensor_scalar(acc[:], acc[:], 1.0, COS[k], ALU.mult, ALU.add)
                    nc.gpsimd.drain()
                    nc.gpsimd.tensor_tensor(acc[:], acc[:], acc[:], ALU.mult)
                    nc.gpsimd.drain()
                    nc.gpsimd.tensor_tensor(RC[:, r, :], acc[:], live[:], ALU.mult).then_inc(s["rc_ready"], 1)
                    nc.gpsimd.drain()

            steps(pool, step)

        def act_rstd(act, q, value, k0, k1):
            act.wait_ge(q["mv_ready"], value)
            nc.scalar.activation(lnv[:, k0:k1, :], mv[:, k0:k1, :, 1], ACT.Ln, bias=EPSC)
            nc.scalar.drain()
            nc.scalar.activation(rstd[:, k0:k1, :], lnv[:, k0:k1, :], ACT.Exp, scale=-0.5).then_inc(q["rs_ready"], 1)

        def act_norm(act, q, value, k, src, dst, done):
            act.wait_ge(q["shift_ready"], value)
            for g in range(G):
                last = nc.scalar.activation(dst[:, g * C:(g + 1) * C], src[:, g * C:(g + 1) * C], ACT.Identity,
                                            bias=shift[:, k, g:g + 1], scale=rstd[:, k, g:g + 1])
            last.then_inc(done, 1)

        def act_a2(act, q, n):
            act.wait_ge(q["a2_mm"], n + 1)
            nc.scalar.copy(pair(A2[:]), T3).then_inc(q["a2_ready"], 1)

        @block.scalar
        def _(act):
            nc.scalar.preload_act_table_set("natural_log_exp_and_others")
            act.wait_ge(v_c1, 1)
            nc.scalar.activation(f0[:, 0:1], noff_c, ACT.Square)
            nc.scalar.drain()
            nc.scalar.activation(f0[:, 1:2], f0[:, 0:1], ACT.Exp, scale=coef_c).then_inc(a_c1, 1)
            act.wait_ge(v_c2, 1)
            nc.scalar.activation(s0[:, 1:2], s0[:, 0:1], ACT.Exp)
            nc.scalar.drain()
            nc.scalar.activation(s0[:, 2:3], s0[:, 1:2], ACT.Ln, bias=0.5, scale=0.5).then_inc(a_c2, 1)

            def step(t, cyc, r):
                n1, n2 = on(t, "N1"), on(t, "N2")
                if on(t, "C1"):
                    act.wait_ge(s["agg_mm"], t - 2)
                    wait(act, s["ow1_mm"], t - 3)
                    nc.scalar.copy(AGG[:], AG[:, 0:G * N]).then_inc(s["agg_ready"], 1)
                if on(t, "A") or on(t, "C1"):
                    wait(act, s["flags_ready"], t)
                if on(t, "A"):
                    act.wait_ge(loadA[r], cyc * 32 + 32)
                    nc.scalar.activation(negs[:], ADJ[:, r, :], ACT.Relu, scale=-1.0,
                                         accum_out=news[:, 0:1]).then_inc(s["neg_ready"], 1)
                if n1 or n2:
                    act_rstd(act, s, t - 3, 0 if n1 else 1, 2 if n2 else 1)
                if on(t, "B1"):
                    rr = turn(cyc, r, 1)[1]
                    act.wait_ge(s["h_mm"], t)
                    nc.scalar.activation(E[:], HH, ACT.Exp, bias=FB1).then_inc(s["e_ready"], 1)
                if on(t, "A"):
                    act.wait_ge(s["y_mm"], t + 1)
                    wait(act, p_ready[2], t - 2)
                    nc.scalar.copy(YT[:, r, 0:2 * G:2, 0:C], pair(M[:, 0:G * C])).then_inc(s["y_ready"], 1)
                if n1:
                    act_norm(act, s, t - 3, 0, Z, X1[:, turn(cyc, r, 4)[1], :], s["x1_ready"])
                if on(t, "C1"):
                    act.wait_ge(s["ow1_mm"], t - 2)
                    nc.scalar.activation(pair(L2[:]), T1, ACT.Exp, bias=OB1, accum_out=news[:, 5:6]).then_inc(s["e2_ready"], 1)
                    wait(act, s["ow2_mm"], t - 3)
                    act.wait_ge(s["e2_ready"], t - 2)
                    nc.scalar.activation(S2[:], L2[:], ACT.Ln, bias=0.5, scale=0.5).then_inc(s["s2_ready"], 1)
                if on(t, "B1"):
                    act.wait_ge(s["e_ready"], t)
                    nc.scalar.activation(S[:, rr, :, :], E[:], ACT.Ln, bias=0.5, scale=0.5).then_inc(s["s_ready"], 1)
                if on(t, "C2"):
                    act_a2(act, s, t - 4)
                if n2:
                    c, rr5 = turn(cyc, r, 5)
                    if not isinstance(t, int) or t - 5 >= RING:
                        act.wait_ge(stored[rr5], c * 16)
                    act_norm(act, s, t - 3, 1, Z2, OUT[:, rr5, :], s["out_ready"])
                if on(t, "A"):
                    act.wait_ge(s["gather_mm"], t + 1)
                    nc.scalar.copy(YT[:, r, 1:2 * G:2, :], GO).then_inc(s["yo_ready"], 1)
                    act.wait_ge(s["slots_ready"], t + 1)
                    wait(act, s["bcast_mm"], t)
                    nc.scalar.copy(VB[:], SV[:, r, 0, :].unsqueeze(2).broadcast_to([N, SLOTS, 32])).then_inc(s["vb_ready"], 1)
                    act.wait_ge(s["bcast_mm"], t + 1)
                    nc.scalar.activation(SQ[:], M[:, 0:GROUPS * N], ACT.Square, bias=noff_c).then_inc(s["sq_ready"], 1)
                    nc.scalar.drain()
                    nc.scalar.activation(FT[:, r, :], SQ[:], ACT.Exp, scale=coef_c).then_inc(s["f_ready"], 1)

            steps(act, step)

            act.wait_ge(flag_ready, 1)
            general = act.value_load(flag_i[0:1, 0:1], min_val=0, max_val=1)
            with act.If(general > 0):
                with act.Fori(0, PAIRS) as n:
                    for g in range(G):
                        act.wait_ge(gs["y_mm"], n * 2 + (g + 1))
                        nc.scalar.copy(YT[:, 0, 0, 0:C], M[:, 0:C]).then_inc(gs["y_ready"], 1)
                        with act.Fori(0, N // PER) as i:
                            m = n * (G * N // PER) + i + g * (N // PER)
                            act.wait_ge(gs["bcast"], m + 1)
                            nc.scalar.activation(SQ[:, 0:N], M[:, 0:N], ACT.Square, bias=noff_c)
                            nc.scalar.drain()
                            nc.scalar.activation(FT[:, 0, 0:N], SQ[:, 0:N], ACT.Exp, scale=coef_c).then_inc(gs["f"], 1)
                            act.wait_ge(gs["hm"], m + 1)
                            nc.scalar.activation(E[:, :, 0:N], E[:, :, 0:N], ACT.Exp)
                            nc.scalar.drain()
                            nc.scalar.activation(E[:, :, 0:N], E[:, :, 0:N], ACT.Ln, bias=0.5, scale=0.5).then_inc(gs["l"], 1)
                    act.wait_ge(gs["hm_ready"], n + 1)
                    nc.scalar.activation(L2[:], HM[:], ACT.Exp)
                    nc.scalar.drain()
                    nc.scalar.activation(L2[:], L2[:], ACT.Ln, bias=0.5, scale=0.5).then_inc(gs["l2_ready"], 1)
                    act_rstd(act, gs, n * 2 + 1, 0, 1)
                    act_norm(act, gs, n * 2 + 1, 0, Z, X1[:, 0, :], gs["x1_ready"])
                    act_a2(act, gs, n)
                    act_rstd(act, gs, n * 2 + 2, 1, 2)
                    act_norm(act, gs, n * 2 + 2, 1, Z2, OUT[:, 0, :], gs["out_ready"])
                act.nop()

        def v_residual(v, q, n, rr):
            v.wait_ge(q["ow2_mm"], n + 1)
            v.wait_ge(q["xb_ready"], n + 1)
            nc.vector.tensor_tensor(pair(Z[:]), T2, pair(XB[:, rr, :]), ALU.add).then_inc(q["z_ready"], 1)

        def v_stats(src, k):
            for g in range(G):
                last = nc.vector.bn_stats(st[:, k, g, :], src[:, g * C:(g + 1) * C])
            return last

        def v_moments(k):
            for g in range(G):
                last = nc.vector.bn_aggr(mv[:, k, g, :], st[:, k, g, :])
            return last

        def v_shift(v, q, value, k0, k1):
            v.wait_ge(q["rs_ready"], value)
            nc.vector.scalar_tensor_tensor(shift[:, k0:k1, :], mv[:, k0:k1, :, 0], -1.0, rstd[:, k0:k1, :],
                                           ALU.mult, ALU.mult).then_inc(q["shift_ready"], 1)

        def v_rn(v, q, n):
            v.wait_ge(q["out_mm"], n + 1)
            nc.vector.reciprocal(rn[:], NS).then_inc(q["rn_ready"], 1)

        def v_scale(v, q, n):
            v.wait_ge(q["rn_ready"], n + 1)
            for g in range(G):
                last = nc.vector.scalar_tensor_tensor(U[:, g * C:(g + 1) * C], T4[:, g, :], rn[:, g:g + 1], bL_bc,
                                                      ALU.mult, ALU.add)
            last.then_inc(q["u_ready"], 1)

        def v_leaky(v, q, n):
            v.wait_ge(q["u_ready"], n + 1)
            nc.vector.scalar_tensor_tensor(V[:], U[:], 0.01, U[:], ALU.mult, ALU.max).then_inc(q["v_ready"], 1)

        @block.vector
        def _(v):
            nc.vector.memset(ones[:], 1.0)
            nc.vector.memset(ones_h[:], 1.0)
            nc.vector.memset(flags[:], 0.0)
            nc.vector.memset(news[:], 0.0)
            nc.vector.memset(YT[:, :, :, C + TAB - 1:C + TAB], 0.0)
            nc.vector.memset(EPSC, EPS)
            v.wait_ge(pool_consts, 2)
            nc.vector.tensor_copy(iota[:], iota_i[:])
            nc.vector.tensor_copy(part[:], part_i[:])
            nc.vector.drain()
            nc.vector.tensor_scalar(ident[:], iota[:], part[:, 0:1], None, ALU.is_equal)
            nc.vector.tensor_scalar(upper[:], iota[:], part[:, 0:1], None, ALU.is_gt)
            nc.vector.tensor_scalar(part5[:], part[:], float(MAIN), None, ALU.add)
            v.wait_ge(c_dma, 32)
            nc.vector.tensor_scalar(noff_c, noff_c, -1.0, None, ALU.mult)
            nc.vector.tensor_tensor(coef_c, width_c, width_c, ALU.mult)
            nc.vector.tensor_scalar(FB1L, FB1, LN2, None, ALU.subtract)
            nc.vector.tensor_scalar(OB1L, OB1, LN2, None, ALU.subtract)
            nc.vector.tensor_copy(hsum[:, R:R + 1], FB1)
            nc.vector.tensor_copy(hsum[:, 0:R], fw1T)
            nc.vector.drain()
            nc.vector.reciprocal(coef_c, coef_c)
            nc.vector.drain()
            nc.vector.tensor_scalar(coef_c, coef_c, -0.5, None, ALU.mult).then_inc(v_c1, 1)
            nc.vector.tensor_reduce(s0[:, 3:4], hsum[:], AX.X, ALU.add, apply_absolute_value=True)
            nc.vector.tensor_copy(b2_hi[:], b2_bc)
            nc.vector.drain()
            nc.vector.tensor_scalar(flags[:, 7:8], s0[:, 3:4], CLAMP, None, ALU.subtract)
            nc.vector.tensor_tensor(b2_res[:], b2_bc, b2_hi[:], ALU.subtract)
            nc.vector.drain()
            nc.vector.tensor_copy(b2_mid[:], b2_res[:])
            nc.vector.drain()
            nc.vector.tensor_tensor(b2_res[:], b2_res[:], b2_mid[:], ALU.subtract)
            nc.vector.tensor_scalar(b2_sel[:], b2_hi[:], ident[:, 0:1], None, ALU.mult)
            nc.vector.drain()
            nc.vector.scalar_tensor_tensor(b2_sel[:], b2_mid[:], ident[:, 1:2], b2_sel[:], ALU.mult, ALU.add)
            nc.vector.drain()
            nc.vector.scalar_tensor_tensor(b2_sel[:], b2_res[:], ident[:, 2:3], b2_sel[:], ALU.mult, ALU.add)
            nc.vector.drain()
            for t in range(PER):
                nc.vector.tensor_copy(b2_rows[:, t, :], b2_sel[:])
            v.wait_ge(pe_c1, 1)
            nc.vector.tensor_scalar(s0[:, 0:1], M[:, 0:1], FB1, CLAMP, ALU.add, ALU.min).then_inc(v_c2, 1)
            v.wait_ge(a_c2, 1)
            nc.vector.scalar_tensor_tensor(s0[:, 3:4], M[:, 0:1], FB1L, s0[:, 2:3], ALU.add, ALU.max)
            nc.vector.drain()
            nc.vector.tensor_scalar(S2[:, 0:N], ones[:], s0[:, 3:4], None, ALU.mult).then_inc(v_c2, 1)
            v.wait_ge(pe_c2, 1)
            nc.vector.tensor_tensor(W0_bc[:], O[:, 0:C], b2_bc, ALU.add)
            nc.vector.drain().then_inc(v_setup, 1)

            def times_y(t, rr, g):
                v.wait_ge(w_mm[g], t - 1)
                wait(v, scat_mm[g], t - 2)
                y = YT[:, rr, :, 0:C]
                if g != 1:
                    y = YT[:, rr, g, 0:C].unsqueeze(1).broadcast_to([N, PER, C])
                nc.vector.tensor_tensor(P[:, g, :].rearrange("p (t c) -> p t c", t=PER),
                                        Wb[:].rearrange("p (t c) -> p t c", t=PER), y, ALU.mult).then_inc(p_ready[g], 1)

            def hot(rr, q):
                last = one_hot(nc.vector, q, SV[:, rr, 1, q:q + 1], RC[:, rr, q:q + 1])
                if q % PER == PER - 1:
                    last.then_inc(oh_ready[q // PER], 1)

            def step(t, cyc, r):
                a, b2, c1, n1, c2, n2 = (on(t, k) for k in ("A", "B2", "C1", "N1", "C2", "N2"))
                rr = turn(cyc, r, 2)[1]
                tab = YT[:, r, 0:2 * G:2, C:C + TAB]
                ovt = YT[:, r, 1:2 * G:2, C:C + TAB]
                adj = pair(ADJ[:, r, :])

                if n1:
                    last = v_stats(Z, 0)
                if n2:
                    v.wait_ge(s["z2_ready"], t - 4)
                    last = v_stats(Z2, 1)
                if n1 or n2:
                    last.then_inc(s["st_ready"], 1)
                if a:
                    v.wait_ge(loadA[r], cyc * 32 + 32)
                    nc.vector.scalar_tensor_tensor(KEY[:], adj, CUTOFF, adj, ALU.is_lt, ALU.mult).then_inc(s["key_ready"], 1)
                    if n1 or n2:
                        v.wait_ge(s["st_ready"], t - 3)
                    wait(v, s["agg_mm"], t - 2)
                    nc.vector.tensor_scalar(M0[:, r, :], ADJ[:, r, :], 0.0, None, ALU.is_equal).then_inc(s["m0_ready"], 1)
                elif n1 or n2:
                    nc.vector.drain()
                if n1:
                    last = v_moments(0)
                if n2:
                    last = v_moments(1)
                if n1 or n2:
                    last.then_inc(s["mv_ready"], 1)
                if b2:
                    v.wait_ge(s["rc_ready"], t - 1)
                    wait(v, scat_mm[0], t - 2)
                    if a:
                        v.wait_ge(s["key_ready"], t + 1)
                    hot(rr, 0)
                elif a:
                    nc.vector.drain()
                if a:
                    for g in range(G):
                        last = nc.vector.max(tab[:, g, 0:8], KEY[:, g, :])
                    last.then_inc(s["top8_ready"], 1)
                if b2:
                    hot(rr, 1)
                    if a:
                        v.wait_ge(s["top8_ready"], t + 1)
                    hot(rr, 2)
                elif a:
                    nc.vector.drain()
                if a:
                    for g in range(G):
                        last = nc.vector.match_replace(KEY2[:, g, :], tab[:, g, 0:8], KEY[:, g, :], -1.0)
                    last.then_inc(s["key2_ready"], 1)
                    for g in range(G):
                        nc.vector.max_index(IDX[:, g, 0:8], tab[:, g, 0:8], KEY[:, g, :])
                if n1 or n2:
                    v_shift(v, s, t - 3, 0 if n1 else 1, 2 if n2 else 1)
                if b2:
                    if a:
                        v.wait_ge(s["key2_ready"], t + 1)
                    hot(rr, 3)
                elif a:
                    nc.vector.drain()
                if a:
                    for g in range(G):
                        last = nc.vector.max(tab[:, g, 8:16], KEY2[:, g, :])
                    last.then_inc(s["top16_ready"], 1)
                if b2:
                    times_y(t, rr, 0)
                if a:
                    v.wait_ge(s["top16_ready"], t + 1)
                    nc.vector.tensor_scalar(over[:], tab[:, :, MAIN:16], 0.0, None, ALU.is_gt).then_inc(s["over_ready"], 1)
                    for g in range(G):
                        last = nc.vector.max_index(IDX[:, g, 8:16], tab[:, g, 8:16], KEY2[:, g, :])
                    last.then_inc(s["idx_ready"], 1)
                    v.wait_ge(s["over_ready"], t + 1)
                    nc.vector.tensor_reduce(cnt[:, r, :], over[:], AX.X, ALU.add).then_inc(s["cnt_ready"], 1)
                if b2:
                    wait(v, scat_mm[1], t - 2)
                    hot(rr, 4)
                    hot(rr, 5)
                if a:
                    v.wait_ge(s["idx_ready"], t + 1)
                    nc.vector.tensor_copy(tab[:, :, 16:32], IDX[:])
                    v.wait_ge(s["rank_mm"], t + 1)
                    nc.vector.tensor_copy(tab[:, :, 32], RANK).then_inc(s["rank_ready"], 1)
                    nc.vector.tensor_copy(news[:, 1:3], tab[:, :, 15])
                if b2:
                    hot(rr, 6)
                if a:
                    v.wait_ge(s["rank_ready"], t + 1)
                    nc.vector.tensor_tensor(end[:], tab[:, :, 32], cnt[:, r, :], ALU.add)
                    for g in range(G):
                        last = nc.vector.tensor_scalar(SELa[:, g, :], iota[:], tab[:, g, 32:33], None, ALU.is_ge)
                    last.then_inc(s["sela_ready"], 1)
                if b2:
                    hot(rr, 7)
                if a:
                    v.wait_ge(s["sela_ready"], t + 1)
                    wait(v, s["gather_mm"], t)
                    for g in range(G):
                        last = nc.vector.scalar_tensor_tensor(SEL[:, g, :], iota[:], end[:, g:g + 1], SELa[:, g, :],
                                                              ALU.is_lt, ALU.mult)
                    last.then_inc(s["sel_ready"], 1)
                    nc.vector.tensor_scalar(news[:, 3:5], end[:], float(N), None, ALU.subtract).then_inc(s["news_ready"], 1)
                if b2:
                    times_y(t, rr, 1)
                if a or c1:
                    if a:
                        v.wait_ge(s["news_ready"], t + 1)
                        v.wait_ge(s["neg_ready"], t + 1)
                    if c1:
                        v.wait_ge(s["e2_ready"], t - 2)
                    nc.vector.tensor_tensor(flags[:, 0:6], flags[:, 0:6], news[:, 0:6], ALU.max).then_inc(s["flags_ready"], 1)
                if a:
                    v.wait_ge(s["yo_ready"], t + 1)
                    nc.vector.tensor_scalar(rel[:], ovt[:, :, 32], part5[:, 0:1], -1.0, ALU.subtract, ALU.mult).then_inc(s["rel_ready"], 1)
                    for g, q in ((0, 0), (1, 8)):
                        nc.vector.tensor_copy(SV[:, r, :, q:q + 4],
                                              tab[:, g, 0:32].rearrange("p (k c) -> p k c", k=2)[:, :, 0:4])
                    nc.vector.tensor_copy(SV[:, r, :, 4:8:2],
                                          tab[:, :, 0:32].rearrange("p g (k c) -> p k g c", k=2)[:, :, :, 4])
                    v.wait_ge(s["rel_ready"], t + 1)
                    nc.vector.tensor_tensor(mask[:], iota[:, 0:16].unsqueeze(1).broadcast_to([N, G, 16]),
                                            rel[:].unsqueeze(2).broadcast_to([N, G, 16]), ALU.is_equal).then_inc(s["mask_ready"], 1)
                if c1:
                    v_residual(v, s, t - 3, turn(cyc, r, 3)[1])
                if a:
                    v.wait_ge(s["mask_ready"], t + 1)
                    nc.vector.tensor_tensor(picked[:], ovt[:, :, 0:32].rearrange("p g (k c) -> p g k c", k=2),
                                            mask[:].unsqueeze(2).broadcast_to([N, G, 2, 16]), ALU.mult).then_inc(s["picked_ready"], 1)
                if c2:
                    v_rn(v, s, t - 4)
                if a:
                    v.wait_ge(s["picked_ready"], t + 1)
                    nc.vector.tensor_reduce(SV[:, r, :, 5:8:2].rearrange("p k g -> p g k"), picked[:],
                                            AX.X, ALU.add).then_inc(s["slots_ready"], 1)
                if c2:
                    v_scale(v, s, t - 4)
                if b2:
                    times_y(t, rr, 2)
                if c2:
                    wait(v, s["z2_ready"], t - 4)
                    v_leaky(v, s, t - 4)

            steps(v, step)

            nc.vector.drain()
            nc.vector.tensor_scalar(flags[:, 5:6], flags[:, 5:6], math.exp(CLAMP), None, ALU.subtract)
            nc.vector.drain()
            nc.vector.tensor_reduce(flag1[:], flags[:], AX.X, ALU.max)
            nc.vector.drain()
            nc.vector.tensor_scalar(flag2[:], flag1[:], 0.0, None, ALU.is_gt).then_inc(flag_v, 1)
            v.wait_ge(flag_pe, 1)
            nc.vector.tensor_scalar(flag_i[:], M[0:1, 0:1], 0.0, None, ALU.is_gt).then_inc(flag_ready, 1)
            v.wait_ge(flag_ready, 1)
            general = v.value_load(flag_i[0:1, 0:1], min_val=0, max_val=1)
            with v.If(general > 0):
                with v.Fori(0, PAIRS) as n:
                    v.wait_ge(g_load, n * 64 + 64)
                    nc.vector.tensor_scalar(g_k[:], ADJ[:, 0, :], 0.1, MAGIC, ALU.mult, ALU.add)
                    nc.vector.drain()
                    nc.vector.tensor_scalar(g_k[:], g_k[:], MAGIC, None, ALU.subtract)
                    nc.vector.drain()
                    nc.vector.scalar_tensor_tensor(g_u[:], g_k[:], -10.0, ADJ[:, 0, :], ALU.mult, ALU.add)
                    nc.vector.drain()
                    nc.vector.tensor_tensor(g_u[:], g_u[:], g_u[:], ALU.mult)
                    nc.vector.drain()
                    nc.vector.tensor_scalar(g_k[:], g_u[:], COS[6], None, ALU.mult)
                    for k in range(5, 0, -1):
                        nc.vector.drain()
                        nc.vector.scalar_tensor_tensor(g_k[:], g_k[:], COS[k], g_u[:], ALU.add, ALU.mult)
                    nc.vector.drain()
                    nc.vector.tensor_scalar(g_k[:], g_k[:], COS[0], None, ALU.add)
                    nc.vector.drain()
                    nc.vector.tensor_tensor(g_k[:], g_k[:], g_k[:], ALU.mult)
                    nc.vector.drain()
                    nc.vector.scalar_tensor_tensor(g_rc[:], ADJ[:, 0, :], CUTOFF, g_k[:], ALU.is_lt, ALU.mult)
                    nc.vector.memset(AGG[:], 0.0)
                    nc.vector.tensor_tensor(pair(XB[:, 0, :]), pair(X[:, 0, :]),
                                            ob2_bc.unsqueeze(1).broadcast_to([N, G, C]), ALU.add).then_inc(gs["xb_ready"], 1)
                    nc.vector.drain()
                    for g in range(G):
                        with v.Fori(0, N // PER) as i:
                            m = n * (G * N // PER) + i + g * (N // PER)
                            nc.vector.tensor_copy(g_val[:], ADJ[:, 0, bass.ds(i * PER + g * N, PER)])
                            nc.vector.tensor_copy(g_w[:], g_rc[:, bass.ds(i * PER + g * N, PER)])
                            nc.vector.tensor_copy(g_idx[:], iota[:, bass.ds(i * PER, PER)])
                            nc.vector.drain()
                            nc.vector.tensor_copy(g_vb[:], g_val[:].unsqueeze(2).broadcast_to([N, PER, 32])).then_inc(gs["pick"], 1)
                            for q in range(PER):
                                one_hot(nc.vector, q, g_idx[:, q:q + 1], g_w[:, q:q + 1])
                            v.wait_ge(gs["h_mm"], m + 1)
                            nc.vector.tensor_scalar(E[:, :, 0:N], H[:, :, 0:N], FB1, CLAMP, ALU.add, ALU.min).then_inc(gs["hm"], 1)
                            v.wait_ge(gs["l"], m + 1)
                            nc.vector.scalar_tensor_tensor(S[:, 0, :, 0:N], H[:, :, 0:N], FB1L, E[:, :, 0:N],
                                                           ALU.add, ALU.max).then_inc(gs["s"], 1)
                            v.wait_ge(gs["y_ready"], n * 2 + (g + 1))
                            v.wait_ge(gs["w_mm"], m + 1)
                            nc.vector.tensor_tensor(P[:, 0, :].rearrange("p (t c) -> p t c", t=PER),
                                                    Wb[:].rearrange("p (t c) -> p t c", t=PER),
                                                    YT[:, 0, 0, 0:C].unsqueeze(1).broadcast_to([N, PER, C]), ALU.mult)
                            nc.vector.drain().then_inc(gs["p"], 1)
                            v.wait_ge(gs["scat"], m + 1)
                            nc.vector.tensor_tensor(AGG[:, g * N:(g + 1) * N], AG[:, 0:N], AGG[:, g * N:(g + 1) * N], ALU.add)
                            nc.vector.drain()
                    nc.vector.drain().then_inc(gs["agg"], 1)
                    v.wait_ge(gs["ow1_mm"], n + 1)
                    nc.vector.tensor_scalar(pair(HM[:]), T1, OB1, CLAMP, ALU.add, ALU.min).then_inc(gs["hm_ready"], 1)
                    v.wait_ge(gs["l2_ready"], n + 1)
                    nc.vector.scalar_tensor_tensor(pair(S2[:]), T1, OB1L, pair(L2[:]), ALU.add, ALU.max).then_inc(gs["s2_ready"], 1)
                    v_residual(v, gs, n, 0)
                    nc.vector.drain()
                    v_stats(Z, 0)
                    nc.vector.drain()
                    v_moments(0).then_inc(gs["mv_ready"], 1)
                    v_shift(v, gs, n * 2 + 1, 0, 1)
                    v_rn(v, gs, n)
                    v_scale(v, gs, n)
                    v_leaky(v, gs, n)
                    nc.vector.drain()
                    nc.vector.tensor_tensor(Z2[:], V[:], X1[:, 0, :], ALU.add)
                    nc.vector.drain()
                    v_stats(Z2, 1)
                    nc.vector.drain()
                    v_moments(1).then_inc(gs["mv_ready"], 1)
                    v_shift(v, gs, n * 2 + 2, 1, 2)
                v.nop()

        def mm(o, w, m, start=True, stop=True):
            return nc.tensor.matmul(o, w, m, start=start, stop=stop)

        def pe_ow1(pe, q, n):
            for g in range(G):
                last = mm(T1[:, g, :], ow1s, AGG[:, g * N:(g + 1) * N])
            last.then_inc(q["ow1_mm"], 1)

        def pe_ow2(pe, q, n):
            pe.wait_ge(q["s2_ready"], n + 1)
            for g in range(G):
                last = mm(T2[:, g, :], S2[:, g * N:(g + 1) * N], ow2s)
            last.then_inc(q["ow2_mm"], 1)

        def pe_agg2(pe, q, n, rr):
            pe.wait_ge(q["x1_ready"], n + 1)
            for g in range(G):
                last = mm(T3[:, g, :], X1[:, rr, g * C:(g + 1) * C], ADJ2[:, rr, g * N:(g + 1) * N])
            last.then_inc(q["a2_mm"], 1)
            for g in range(G):
                last = mm(NS[:, g:g + 1], ADJ2[:, rr, g * N:(g + 1) * N], ones[:, 0:1])
            last.then_inc(q["ns_mm"], 1)

        def pe_out(pe, q, n):
            pe.wait_ge(q["a2_ready"], n + 1)
            for g in range(G):
                last = mm(T4[:, g, :], A2[:, g * N:(g + 1) * N], WTs)
            last.then_inc(q["out_mm"], 1)

        def filter_out(rr, g, src):
            mm(Wb[:], ones_h[:], b2_rows[:].rearrange("p t c -> p (t c)"), stop=False)
            for t in range(PER):
                last = mm(Wb[:, t * C:(t + 1) * C], src[:, rr, t, g * N:(g + 1) * N], fw2s, start=False, stop=(t == PER - 1))
            return last

        @block.tensor
        def _(pe):
            pe.wait_ge(a_c1, 1)
            mm(M[:, 0:1], fw1s[0:R, :], f0[0:R, 1:2]).then_inc(pe_c1, 1)
            pe.wait_ge(v_c2, 2)
            mm(O[:, 0:C], S2[:, 0:N], fw2s).then_inc(pe_c2, 1)
            pe.wait_ge(v_setup, 1)

            def w_group(t, rr, g):
                pe.wait_ge(s["s_ready"], t - 1)
                if g:
                    pe.wait_ge(p_ready[g - 1], t - 1)
                else:
                    wait(pe, p_ready[GROUPS - 1], t - 2)
                filter_out(rr, g, S).then_inc(w_mm[g], 1)

            def scatter(t, rr, g):
                pe.wait_ge(p_ready[g], t - 1)
                if PER * g + PER - 1 in POOL_HOT:
                    pe.wait_ge(oh_pool, t - 1)
                else:
                    pe.wait_ge(oh_ready[g], t - 1)
                for i in range(PER):
                    q = PER * g + i
                    h = GRAPH_OF[q]
                    if q == MAIN + 1:
                        zeros(t, rr, 0)
                    last = mm(AG[:, h * N:(h + 1) * N], P[:, g, i * C:(i + 1) * C], OH[:, q, :],
                              start=(q in (0, MAIN + 1)), stop=False)
                last.then_inc(scat_mm[g], 1)

            def zeros(t, rr, h):
                return mm(AG[:, h * N:(h + 1) * N], YW0[:, rr, h, :], M0[:, rr, h * N:(h + 1) * N], start=False)

            def step(t, cyc, r):
                r1, r2, r4 = turn(cyc, r, 1)[1], turn(cyc, r, 2)[1], turn(cyc, r, 4)[1]
                wait(pe, s["z_ready"], min(t - 3, PAIRS) if isinstance(t, int) else t - 3)
                wait(pe, s["u_ready"], t - 4)
                if on(t, "B1"):
                    pe.wait_ge(s["f_ready"], t)
                    for i in range(PER):
                        last = mm(H[:, i, 0:GROUPS * N], fw1s[32 * i:32 * i + R, :], FT[32 * i:32 * i + R, r1, :])
                    last.then_inc(s["h_mm"], 1)
                if on(t, "A"):
                    pe.wait_ge(loadA[r], cyc * 32 + 32)
                    wait(pe, s["sq_ready"], t)
                    for g in range(G):
                        last = mm(M[:, g * C:(g + 1) * C], XT[:, r, g * N:(g + 1) * N], win)
                    last.then_inc(s["y_mm"], 1)
                if on(t, "B2"):
                    w_group(t, r2, 0)
                if on(t, "B1"):
                    pe.wait_ge(s["e_ready"], t)
                if on(t, "C1"):
                    pe.wait_ge(s["agg_ready"], t - 2)
                    pe_ow1(pe, s, t - 3)
                if on(t, "B2"):
                    w_group(t, r2, 1)
                if on(t, "A"):
                    pe.wait_ge(s["cnt_ready"], t + 1)
                    pe.wait_ge(s["y_ready"], t + 1)
                    mm(RANK, upper[:], cnt[:, r, :]).then_inc(s["rank_mm"], 1)
                if on(t, "C2"):
                    pe.wait_ge(loadD[r4], turn(cyc, r, 4)[0] * 16 + 16)
                    pe_agg2(pe, s, t - 4, r4)
                if on(t, "B2"):
                    wait(pe, s["agg_ready"], t - 2)
                    scatter(t, r2, 0)
                if on(t, "A"):
                    pe.wait_ge(s["sel_ready"], t + 1)
                    wait(pe, s["yo_ready"], t)
                    for g in range(G):
                        last = mm(GO[:, g, :], SEL[:, g, :], YT[:, r, 2 * g, :])
                    last.then_inc(s["gather_mm"], 1)
                if on(t, "C1"):
                    pe_ow2(pe, s, t - 3)
                if on(t, "B2"):
                    w_group(t, r2, 2)
                if on(t, "C2"):
                    pe_out(pe, s, t - 4)
                if on(t, "B2"):
                    pe.wait_ge(s["yw0_ready"], t - 1)
                    pe.wait_ge(s["m0_ready"], t - 1)
                    scatter(t, r2, 1)
                if on(t, "A"):
                    pe.wait_ge(s["vb_ready"], t + 1)
                    for g in range(GROUPS):
                        src = VB[:, PER * g:PER * g + PER, :].rearrange("p t r -> p (t r)")
                        last = nc.tensor.transpose(M[:, g * N:(g + 1) * N], src, ident[:])
                    last.then_inc(s["bcast_mm"], 1)
                if on(t, "B2"):
                    scatter(t, r2, 2)
                    zeros(t, r2, 1).then_inc(s["agg_mm"], 1)

            steps(pe, step)

            pe.wait_ge(flag_v, 1)
            mm(M[0:1, 0:1], flag2[:], ones[:, 0:1]).then_inc(flag_pe, 1)
            pe.wait_ge(flag_ready, 1)
            general = pe.value_load(flag_i[0:1, 0:1], min_val=0, max_val=1)
            with pe.If(general > 0):
                with pe.Fori(0, PAIRS) as n:
                    pe.wait_ge(g_load, n * 64 + 64)
                    for g in range(G):
                        mm(M[:, 0:C], XT[:, 0, g * N:(g + 1) * N], win).then_inc(gs["y_mm"], 1)
                        with pe.Fori(0, N // PER) as i:
                            m = n * (G * N // PER) + i + g * (N // PER)
                            pe.wait_ge(gs["pick"], m + 1)
                            pe.wait_ge(gs["y_ready"], n * 2 + (g + 1))
                            nc.tensor.transpose(M[:, 0:N], g_vb[:].rearrange("p t r -> p (t r)"), ident[:]).then_inc(gs["bcast"], 1)
                            pe.wait_ge(gs["f"], m + 1)
                            for k in range(PER):
                                last = mm(H[:, k, 0:N], fw1s[32 * k:32 * k + R, :], FT[32 * k:32 * k + R, 0, 0:N])
                            last.then_inc(gs["h_mm"], 1)
                            pe.wait_ge(gs["s"], m + 1)
                            filter_out(0, 0, S).then_inc(gs["w_mm"], 1)
                            pe.wait_ge(gs["p"], m + 1)
                            for k in range(PER):
                                last = mm(AG[:, 0:N], P[:, 0, k * C:(k + 1) * C], OH[:, k, :], start=(k == 0), stop=(k == PER - 1))
                            last.then_inc(gs["scat"], 1)
                    pe.wait_ge(gs["agg"], n + 1)
                    pe_ow1(pe, gs, n)
                    pe_ow2(pe, gs, n)
                    pe_agg2(pe, gs, n, 0)
                    pe_out(pe, gs, n)
                pe.nop()


def kernel(**inputs):
    import numpy as _np
    import concourse.bacc as _bacc
    from concourse import mybir as _mybir
    from concourse.bass_utils import run_bass_kernel_spmd as _run

    def pairs(a):
        return a.reshape(PAIRS, G, N, N).transpose(0, 2, 1, 3).reshape(PAIRS, N, G * N)

    def col(a):
        return a.reshape(-1, 1)

    given = {k.replace("_gnn", ""): _np.asarray(v) for k, v in inputs.items()}
    x, adj, fw1 = given["x"], given["adj"], given["L0_fw1"]

    def strips(a, fill):
        return _np.pad(a, ((0, 32 - R), (0, 0)), constant_values=fill)[None].repeat(N // 32, 0).reshape(N, a.shape[1])

    layouts = {
        "x": pairs(x),
        "xT": pairs(x.transpose(0, 2, 1)),
        "adjT": pairs(adj.transpose(0, 2, 1)),
        "weights": _np.concatenate([
            given["L0_w_in2f"], given["L0_fw2"], given["L0_ow1"], given["L0_ow2"], given["L1_W"].T, strips(fw1, 0),
            col(given["L0_fb1"]), col(given["L0_ob1"]), strips(col(given["L0_widths"]), 1), strips(col(given["L0_offsets"]), 0),
            fw1.T], axis=1),
        "biases": _np.concatenate([given["L0_fb2"], given["L0_ob2"], given["L1_b"]]),
    }
    nc = _bacc.Bacc("TRN2", target_bir_lowering=False, num_devices=1)
    arrays, args = {}, []
    for name, a in layouts.items():
        a = _np.ascontiguousarray(a)
        arrays[f"in_{name}"] = a
        args.append(nc.dram_tensor(f"in_{name}", a.shape, _mybir.dt.from_np(a.dtype), kind="ExternalInput").ap())
    args.append(nc.dram_tensor("result", (PAIRS, N, G * C), _mybir.dt.float32, kind="ExternalOutput").ap())
    build(nc, *args)
    r = _run(nc, [arrays], core_ids=[0])
    got = r.results[0]["result"]
    return _np.ascontiguousarray(got.reshape(PAIRS, N, G, C).transpose(0, 2, 1, 3).reshape(B, N, C))
```

```python
import math
from contextlib import ExitStack

import concourse.bass as bass
from concourse import mybir

F32 = mybir.dt.float32
BF16 = mybir.dt.bfloat16
U32 = mybir.dt.uint32
I32 = mybir.dt.int32
ALU = mybir.AluOpType
ACT = mybir.ActivationFunctionType
AX = mybir.AxisListType

B, N, C, R = 64, 128, 128, 20
PAIRS = B // 2
G = 2
TAB = 34
MAIN = 5
SLOTS = G * (MAIN + 1)
GROUPS, PER = SLOTS // 4, 4
RING = 3
UNROLL = 2 * RING
PACKED = 6 * C + 4 + R
CUTOFF = 5.0
LN2 = math.log(2.0)
CLAMP = 40.0
EPS = 1e-5
MAGIC = 1.5 * 2.0 ** 23
COS = [(-1.0) ** k * (math.pi / 10) ** (2 * k) / math.factorial(2 * k) for k in range(7)]
GRAPH_OF = [0, 0, 0, 0, 0, 0, 1, 1, 1, 1, 1, 1]


def build(nc, x, xT, adj, adjT, weights, biases, out):
    ctx = ExitStack()
    with ctx:
        def sb(name, shape, dt=F32):
            return ctx.enter_context(nc.sbuf_tensor(name, shape, dt))

        def pb(name, shape):
            return ctx.enter_context(nc.psum_tensor(name, shape, F32))

        def sem(name):
            return ctx.enter_context(nc.semaphore(name))

        iota_i = sb("iota_i", [N, N], I32)
        part_i = sb("part_i", [N, 1], I32)
        iota = sb("iota", [N, N])
        part = sb("part", [N, 1])
        part5 = sb("part5", [N, 1])
        ident = sb("ident", [N, N])
        upper = sb("upper", [N, N], BF16)
        ones = sb("ones", [N, N])
        ones_h = sb("ones_h", [N, N], BF16)
        packed = sb("packed", [N, PACKED])
        win, fw2s, ow1s, ow2s, WTs = (packed[:, k * C:(k + 1) * C] for k in range(5))
        fw1s = packed[:, 5 * C:6 * C]
        FB1, OB1, width_c, noff_c = (packed[:, 6 * C + k:6 * C + k + 1] for k in range(4))
        fw1T = packed[:, 6 * C + 4:6 * C + 4 + R]
        cols = sb("cols", [C, 4])
        FB1L, OB1L, EPSC, coef_c = (cols[:, k:k + 1] for k in range(4))
        rows = sb("rows", [N, 3 * C])
        b2_bc, ob2_bc, bL_bc = (rows[:, k * C:(k + 1) * C] for k in range(3))
        b2_hi = sb("b2_hi", [N, C], BF16)
        b2_mid = sb("b2_mid", [N, C], BF16)
        b2_res = sb("b2_res", [N, C])
        b2_sel = sb("b2_sel", [N, C])
        b2_rows = sb("b2_rows", [N, PER, C], BF16)
        W0_bc = sb("W0_bc", [N, C])
        f0 = sb("f0", [N, 2])
        s0 = sb("s0", [C, 4])
        hsum = sb("hsum", [C, R + 1])

        ADJ = sb("ADJ", [N, UNROLL, G * N])
        XT = sb("XT", [C, RING, G * N])
        KEY = sb("KEY", [N, G, N])
        KEY2 = sb("KEY2", [N, G, N])
        IDX = sb("IDX", [N, G, 16], U32)
        over = sb("over", [N, G, 16 - MAIN])
        cnt = sb("cnt", [N, RING, G], BF16)
        end = sb("end", [N, G])
        SEL = sb("SEL", [N, G, N])
        SELa = sb("SELa", [N, G, N])
        rel = sb("rel", [N, G])
        mask = sb("mask", [N, G, 16])
        picked = sb("picked", [N, G, 2, 16])
        SV = sb("SV", [N, RING, 2, SLOTS])
        RC = sb("RC", [N, RING, SLOTS])
        VB = sb("VB", [N, SLOTS, 32])
        usq = sb("usq", [N, SLOTS])
        acc = sb("acc", [N, SLOTS])
        live = sb("live", [N, SLOTS])
        YT = sb("YT", [N, RING, 2 * G, C + TAB])
        M0 = sb("M0", [N, RING, G * N])
        YW0 = sb("YW0", [N, RING, G, C])
        SQ = sb("SQ", [N, GROUPS * N])
        FT = sb("FT", [N, RING, GROUPS * N])
        negs = sb("negs", [N, G * N])
        news = sb("news", [N, 8])
        flags = sb("flags", [N, 8])
        E = sb("E", [C, PER, GROUPS * N])
        S = sb("S", [C, RING, PER, GROUPS * N])
        P = sb("P", [N, GROUPS, PER * C])
        OH = sb("OH", [N, SLOTS, N])
        AGG = sb("AGG", [C, G * N])
        X = sb("X", [N, RING, G * C])
        XB = sb("XB", [N, RING, G * C])
        HM = sb("HM", [C, G * N])
        L2 = sb("L2", [C, G * N])
        S2 = sb("S2", [C, G * N])
        Z = sb("Z", [N, G * C])
        st = sb("st", [N, 2, G, 6])
        mv = sb("mv", [N, 2, G, 2])
        lnv = sb("lnv", [N, 2, G])
        rstd = sb("rstd", [N, 2, G])
        shift = sb("shift", [N, 2, G])
        X1 = sb("X1", [N, RING, G * C])
        ADN = sb("ADN", [N, RING, G * N])
        scrap = sb("scrap", [N, G * N])
        ns = sb("ns", [N, G])
        A2 = sb("A2", [C, G * N])
        rn = sb("rn", [N, G])
        U = sb("U", [N, G * C])
        V = sb("V", [N, G * C])
        Z2 = sb("Z2", [N, G * C])
        OUT = sb("OUT", [N, RING, G * C])
        g_rc = sb("g_rc", [N, G * N])
        g_k = sb("g_k", [N, G * N])
        g_u = sb("g_u", [N, G * N])
        g_val = sb("g_val", [N, PER])
        g_vb = sb("g_vb", [N, PER, 32])
        g_idx = sb("g_idx", [N, PER])
        g_w = sb("g_w", [N, PER])
        flag1 = sb("flag1", [N, 1])
        flag2 = sb("flag2", [N, 1])
        flag_i = sb("flag_i", [1, 1], I32)

        H = pb("H", [N, PER, 512])
        Wb = [pb(f"Wb{k}", [N, PER * C]) for k in range(2)]
        AG = pb("AG", [N, 512])
        M = pb("M", [N, 512])
        HH = H[:, :, 0:GROUPS * N]
        T1, T2, T3, T4 = (H[:, k, 0:G * N].rearrange("p (g c) -> p g c", g=G) for k in range(4))
        RANK = M[:, 504:506]
        GO = M[:, 0:G * (C + TAB)].rearrange("p (g c) -> p g c", g=G)

        def pair(t):
            return t.rearrange("p (g c) -> p g c", g=G)

        c_dma = sem("c_dma")
        pool_consts = sem("pool_consts")
        v_consts = sem("v_consts")
        v_c1 = sem("v_c1")
        v_c2 = sem("v_c2")
        a_c1 = sem("a_c1")
        a_c2 = sem("a_c2")
        pe_c1 = sem("pe_c1")
        pe_c2 = sem("pe_c2")
        v_setup = sem("v_setup")
        loadA = [sem(f"loadA{r}") for r in range(UNROLL)]
        loadX = [sem(f"loadX{r}") for r in range(RING)]
        loadD = [sem(f"loadD{r}") for r in range(RING)]
        stored = [sem(f"stored{r}") for r in range(RING)]
        names = ("key_ready top8_ready key2_ready top16_ready over_ready idx_ready cnt_ready news_ready rank_mm rank_ready sela_ready sel_ready "
                 "y_mm y_ready gather_mm yo_ready rel_ready mask_ready picked_ready slots_ready vb_ready "
                 "m0_ready yw0_ready rc_ready bcast_mm sq_ready f_ready neg_ready h_mm hb_mm e_ready s_ready "
                 "agg_mm agg_ready ow1_mm e2_ready s2_ready ow2_mm xb_ready z_ready "
                 "x1_ready a2_mm ns_ready a2_ready out_mm rn_ready u_ready v_ready z2_ready out_ready "
                 "flags_ready st_ready mv_ready rs_ready shift_ready").split()
        s = {k: sem(k) for k in names}
        w_mm = [sem(f"w_mm{g}") for g in range(GROUPS)]
        p_ready = [sem(f"p_ready{g}") for g in range(GROUPS)]
        oh_ready = [sem(f"oh_ready{g}") for g in range(GROUPS)]
        scat_mm = [sem(f"scat_mm{g}") for g in range(GROUPS)]
        oh_pool = sem("oh_pool")
        own = sem("own")
        flag_v = sem("flag_v")
        flag_pe = sem("flag_pe")
        flag_ready = sem("flag_ready")
        g_load = sem("g_load")
        g_stored = sem("g_stored")
        g_pair_done = sem("g_pair_done")
        gnames = ("rc y_mm y_ready pick bcast f h_mm hm l s w_mm p scat add agg "
                  "ow1_mm hm_ready l2_ready s2_ready ow2_mm z_ready xb_ready "
                  "x1_ready a2_mm ns_ready a2_ready out_mm rn_ready u_ready v_ready out_ready mv_ready rs_ready shift_ready").split()
        gs = {k: sem("g_" + k) for k in gnames}

        def wait(eng, which, value):
            if not isinstance(value, int) or value > 0:
                eng.wait_ge(which, value)

        block = ctx.enter_context(nc.Block())

        LAG = {"A": 0, "B1": 1, "B2": 2, "C1": 3, "N1": 4, "C2": 4, "N2": 5}
        AHEAD = 2

        def steps(eng, step, lag=LAG["N2"]):
            first = lag + 1
            rolls = (PAIRS - first) // UNROLL
            for t in range(first):
                step(t, t // UNROLL, t % UNROLL)
            with eng.Fori(0, rolls) as q:
                for k in range(UNROLL):
                    c = first + k
                    step(q * UNROLL + c, q + c // UNROLL, c % UNROLL)
            for t in range(first + UNROLL * rolls, PAIRS + lag):
                step(t, t // UNROLL, t % UNROLL)

        def on(t, stage):
            return not isinstance(t, int) or 0 <= t - LAG[stage] < PAIRS

        def w_bank(r, g):
            return (GROUPS * r + g) % 2

        def slot(r, lag=0):
            return (r - lag) % RING

        def turn(cyc, r, lag, ring=RING):
            return cyc * (UNROLL // ring) + (r - lag) // ring, (r - lag) % ring

        def load_a(sp, n, r):
            wait(sp, s["y_mm"], n - 2)
            sp.dma_start(XT[:, slot(r), :], xT[n]).then_inc(loadA[r], 16)
            wait(sp, s["key_ready"], n - 5)
            wait(sp, s["m0_ready"], n - 5)
            wait(sp, s["neg_ready"], n - 5)
            wait(sp, s["a2_mm"], n - 5)
            sp.dma_start(ADJ[:, r, :], adjT[n]).then_inc(loadA[r], 16)

        def load_x(sp, n, r):
            wait(sp, s["xb_ready"], n - 2)
            sp.dma_start(X[:, r, :], x[n]).then_inc(loadX[r], 16)

        def load_d(sp, n, r):
            wait(sp, s["ns_ready"], n - 2)
            sp.dma_start(ADN[:, r, :], adj[n]).then_inc(loadD[r], 16)

        @block.sync
        def _(sp):
            sp.dma_start(ADJ[:, 0, :], adjT[0]).then_inc(loadA[0], 16)
            sp.dma_start(packed[:], weights).then_inc(c_dma, 16)
            sp.dma_start(XT[:, 0, :], xT[0]).then_inc(loadA[0], 16)
            sp.dma_start(rows[:], biases.partition_broadcast(N)).then_inc(c_dma, 16)

            def step(t, cyc, r):
                def has(lag):
                    return not isinstance(t, int) or 0 <= t - lag < PAIRS

                if has(0) and not (isinstance(t, int) and t == 0):
                    load_a(sp, t, r)
                if has(LAG["C1"]):
                    load_x(sp, t - LAG["C1"], slot(r, LAG["C1"]))
                if has(LAG["C2"]):
                    load_d(sp, t - LAG["C2"], slot(r, LAG["C2"]))
                lag = LAG["N2"] + AHEAD
                if has(lag):
                    rr = turn(cyc, r, lag)[1]
                    wait(sp, s["out_ready"], t - lag + 1)
                    sp.dma_start(out[t - lag], OUT[:, rr, :]).then_inc(stored[rr], 16)

            steps(sp, step, LAG["N2"] + AHEAD)
            for r in range(RING):
                sp.wait_ge(stored[r], 16 * ((PAIRS - r + RING - 1) // RING))
            sp.wait_ge(flag_ready, 1)
            general = sp.value_load(flag_i[0:1, 0:1], min_val=0, max_val=1)
            with sp.If(general > 0):
                with sp.Fori(0, PAIRS) as n:
                    sp.dma_start(ADJ[:, 0, :], adjT[n]).then_inc(g_load, 16)
                    sp.dma_start(ADN[:, 0, :], adj[n]).then_inc(g_load, 16)
                    sp.dma_start(XT[:, 0, :], xT[n]).then_inc(g_load, 16)
                    sp.dma_start(X[:, 0, :], x[n]).then_inc(g_load, 16)
                    sp.wait_ge(gs["out_ready"], n + 1)
                    sp.dma_start(out[n], OUT[:, 0, :]).then_inc(g_stored, 16)
                    sp.wait_ge(g_stored, n * 16 + 16)
                    sp.sem_inc(g_pair_done, 1)
                sp.nop()

        POOL_HOT = range(8, 12)

        def one_hot(eng, q, idx, w):
            return eng.tensor_scalar(OH[:, q, :], iota[:], idx, w, ALU.is_equal, ALU.mult)

        @block.gpsimd
        def _(pool):
            nc.gpsimd.iota(iota_i[:], pattern=[[1, N]], base=0, channel_multiplier=0).then_inc(pool_consts, 1)
            nc.gpsimd.iota(part_i[:], pattern=[[1, 1]], base=0, channel_multiplier=1).then_inc(pool_consts, 1)
            pool.wait_ge(c_dma, 32)

            def step(t, cyc, r):
                if on(t, "B2"):
                    wait(pool, scat_mm[2], t - 2)
                if on(t, "C1"):
                    c, rr = turn(cyc, r, 3)
                    wait(pool, loadX[rr], c * 16 + 16)
                    nc.gpsimd.tensor_tensor(pair(XB[:, rr, :]), pair(X[:, rr, :]),
                                            ob2_bc.unsqueeze(1).broadcast_to([N, G, C]), ALU.add).then_inc(s["xb_ready"], 1)
                if on(t, "B2"):
                    rr = slot(r, 2)
                    for q in POOL_HOT:
                        last = one_hot(nc.gpsimd, q, SV[:, rr, 1, q:q + 1], RC[:, rr, q:q + 1])
                    last.then_inc(oh_pool, 1)
                if on(t, "C2"):
                    rr = slot(r, 4)
                    wait(pool, s["v_ready"], t - 3)
                    wait(pool, s["out_ready"], t - 4)
                    nc.gpsimd.tensor_tensor(Z2[:], V[:], X1[:, rr, :], ALU.add).then_inc(s["z2_ready"], 1)
                if on(t, "A"):
                    wait(pool, s["slots_ready"], t + 1)
                    val = SV[:, slot(r), 0, :]
                    nc.gpsimd.tensor_tensor(usq[:], val, val, ALU.mult)
                    nc.gpsimd.tensor_scalar(live[:], val, 0.0, None, ALU.is_gt)
                    nc.gpsimd.drain()
                    nc.gpsimd.tensor_scalar(acc[:], usq[:], COS[6], COS[5], ALU.mult, ALU.add)
                    for k in range(4, -1, -1):
                        nc.gpsimd.drain()
                        nc.gpsimd.tensor_tensor(acc[:], acc[:], usq[:], ALU.mult)
                        nc.gpsimd.drain()
                        nc.gpsimd.tensor_scalar(acc[:], acc[:], 1.0, COS[k], ALU.mult, ALU.add)
                    nc.gpsimd.drain()
                    nc.gpsimd.tensor_tensor(acc[:], acc[:], acc[:], ALU.mult)
                    nc.gpsimd.drain()
                    nc.gpsimd.tensor_tensor(RC[:, slot(r), :], acc[:], live[:], ALU.mult).then_inc(s["rc_ready"], 1)
                    if isinstance(t, int) and t == 0:
                        pool.wait_ge(v_setup, 1)
                    wait(pool, s["agg_mm"], t - 2)
                    wait(pool, s["y_ready"], t + 1)
                    nc.gpsimd.tensor_tensor(YW0[:, slot(r), :, :], YT[:, slot(r), 0:2 * G:2, 0:C],
                                            W0_bc[:].unsqueeze(1).broadcast_to([N, G, C]), ALU.mult).then_inc(s["yw0_ready"], 1)
                    nc.gpsimd.drain()

            steps(pool, step)

        def act_rstd(act, q, value, k0, k1):
            act.wait_ge(q["mv_ready"], value)
            nc.scalar.activation(lnv[:, k0:k1, :], mv[:, k0:k1, :, 1], ACT.Ln, bias=EPSC)
            nc.scalar.drain()
            nc.scalar.activation(rstd[:, k0:k1, :], lnv[:, k0:k1, :], ACT.Exp, scale=-0.5).then_inc(q["rs_ready"], 1)

        def act_norm(act, q, value, k, src, dst, done):
            act.wait_ge(q["shift_ready"], value)
            for g in range(G):
                last = nc.scalar.activation(dst[:, g * C:(g + 1) * C], src[:, g * C:(g + 1) * C], ACT.Identity,
                                            bias=shift[:, k, g:g + 1], scale=rstd[:, k, g:g + 1])
            last.then_inc(done, 1)

        def act_rowsum(act, q, n, rr):
            wait(act, q["rn_ready"], n)
            for g in range(G):
                last = nc.scalar.activation(scrap[:, g * N:(g + 1) * N], ADN[:, rr, g * N:(g + 1) * N], ACT.Identity, accum_out=ns[:, g:g + 1])
            last.then_inc(q["ns_ready"], 1)

        def act_a2(act, q, n):
            act.wait_ge(q["a2_mm"], n + 1)
            nc.scalar.copy(pair(A2[:]), T3).then_inc(q["a2_ready"], 1)

        @block.scalar
        def _(act):
            nc.scalar.preload_act_table_set("natural_log_exp_and_others")
            act.wait_ge(v_c1, 1)

            def w0():
                nc.scalar.activation(f0[:, 0:1], noff_c, ACT.Square)
                nc.scalar.drain()
                nc.scalar.activation(f0[:, 1:2], f0[:, 0:1], ACT.Exp, scale=coef_c).then_inc(a_c1, 1)
                act.wait_ge(v_c2, 1)
                nc.scalar.activation(s0[:, 1:2], s0[:, 0:1], ACT.Exp)
                nc.scalar.drain()
                nc.scalar.activation(s0[:, 2:3], s0[:, 1:2], ACT.Ln, bias=0.5, scale=0.5).then_inc(a_c2, 1)

            def step(t, cyc, r):
                n1, n2 = on(t, "N1"), on(t, "N2")
                if on(t, "C1"):
                    act.wait_ge(s["agg_mm"], t - 2)
                    wait(act, s["ow1_mm"], t - 3)
                    nc.scalar.copy(AGG[:], AG[:, 0:G * N]).then_inc(s["agg_ready"], 1)
                if on(t, "A") or on(t, "C1"):
                    wait(act, s["flags_ready"], t)
                if on(t, "A"):
                    c, ra = turn(cyc, r, 0, UNROLL)
                    act.wait_ge(loadA[ra], c * 32 + 32)
                    nc.scalar.activation(negs[:], ADJ[:, ra, :], ACT.Relu, scale=-1.0,
                                         accum_out=news[:, 0:1]).then_inc(s["neg_ready"], 1)
                if on(t, "C2"):
                    c, rr = turn(cyc, r, 4)
                    act.wait_ge(loadD[rr], c * 16 + 16)
                    act_rowsum(act, s, t - 4, rr)
                if on(t, "A"):
                    act.wait_ge(s["y_mm"], t + 1)
                    wait(act, p_ready[2], t - 2)
                    nc.scalar.copy(YT[:, slot(r), 0:2 * G:2, 0:C], pair(M[:, 0:G * C])).then_inc(s["y_ready"], 1)
                if n1 or n2:
                    act_rstd(act, s, t - 3, 0 if n1 else 1, 2 if n2 else 1)
                if on(t, "B1"):
                    act.wait_ge(s["h_mm"], t)
                    nc.scalar.activation(E[:, 0:2, :], HH[:, 0:2, :], ACT.Exp, bias=FB1)
                    act.wait_ge(s["hb_mm"], t)
                    nc.scalar.activation(E[:, 2:PER, :], HH[:, 2:PER, :], ACT.Exp, bias=FB1).then_inc(s["e_ready"], 1)
                if n1:
                    act_norm(act, s, t - 3, 0, Z, X1[:, slot(r, 4), :], s["x1_ready"])
                if n2:
                    c, rr = turn(cyc, r, 5)
                    if not isinstance(t, int) or t - 5 >= RING:
                        act.wait_ge(stored[rr], c * 16)
                    act_norm(act, s, t - 3, 1, Z2, OUT[:, rr, :], s["out_ready"])
                if on(t, "C1"):
                    act.wait_ge(s["ow1_mm"], t - 2)
                    nc.scalar.activation(pair(L2[:]), T1, ACT.Exp, bias=OB1, accum_out=news[:, 5:6]).then_inc(s["e2_ready"], 1)
                    wait(act, s["ow2_mm"], t - 3)
                    act.wait_ge(s["e2_ready"], t - 2)
                    nc.scalar.activation(S2[:], L2[:], ACT.Ln, bias=0.5, scale=0.5).then_inc(s["s2_ready"], 1)
                if on(t, "C2"):
                    act_a2(act, s, t - 4)
                if on(t, "A"):
                    act.wait_ge(s["gather_mm"], t + 1)
                    nc.scalar.copy(YT[:, slot(r), 1:2 * G:2, :], GO).then_inc(s["yo_ready"], 1)
                if on(t, "B1"):
                    act.wait_ge(s["e_ready"], t)
                    nc.scalar.activation(S[:, slot(r, 1), :, :], E[:], ACT.Ln, bias=0.5, scale=0.5).then_inc(s["s_ready"], 1)
                if on(t, "A"):
                    act.wait_ge(s["slots_ready"], t + 1)
                    wait(act, s["bcast_mm"], t)
                    nc.scalar.copy(VB[:], SV[:, slot(r), 0, :].unsqueeze(2).broadcast_to([N, SLOTS, 32])).then_inc(s["vb_ready"], 1)
                    act.wait_ge(s["bcast_mm"], t + 1)
                    nc.scalar.activation(SQ[:], M[:, 0:GROUPS * N], ACT.Square, bias=noff_c).then_inc(s["sq_ready"], 1)
                    nc.scalar.drain()
                    nc.scalar.activation(FT[:, slot(r), :], SQ[:], ACT.Exp, scale=coef_c).then_inc(s["f_ready"], 1)
                if isinstance(t, int) and t == 0:
                    w0()

            steps(act, step)

            act.wait_ge(flag_ready, 1)
            general = act.value_load(flag_i[0:1, 0:1], min_val=0, max_val=1)
            with act.If(general > 0):
                with act.Fori(0, PAIRS) as n:
                    act.wait_ge(g_load, n * 64 + 64)
                    for g in range(G):
                        act.wait_ge(gs["y_mm"], n * 2 + (g + 1))
                        nc.scalar.copy(YT[:, 0, 0, 0:C], M[:, 0:C]).then_inc(gs["y_ready"], 1)
                        with act.Fori(0, N // PER) as i:
                            m = n * (G * N // PER) + i + g * (N // PER)
                            act.wait_ge(gs["bcast"], m + 1)
                            nc.scalar.activation(SQ[:, 0:N], M[:, 0:N], ACT.Square, bias=noff_c)
                            nc.scalar.drain()
                            nc.scalar.activation(FT[:, 0, 0:N], SQ[:, 0:N], ACT.Exp, scale=coef_c).then_inc(gs["f"], 1)
                            act.wait_ge(gs["hm"], m + 1)
                            nc.scalar.activation(E[:, :, 0:N], E[:, :, 0:N], ACT.Exp)
                            nc.scalar.drain()
                            nc.scalar.activation(E[:, :, 0:N], E[:, :, 0:N], ACT.Ln, bias=0.5, scale=0.5).then_inc(gs["l"], 1)
                    act.wait_ge(gs["hm_ready"], n + 1)
                    nc.scalar.activation(L2[:], HM[:], ACT.Exp)
                    nc.scalar.drain()
                    nc.scalar.activation(L2[:], L2[:], ACT.Ln, bias=0.5, scale=0.5).then_inc(gs["l2_ready"], 1)
                    act_rstd(act, gs, n * 2 + 1, 0, 1)
                    act_norm(act, gs, n * 2 + 1, 0, Z, X1[:, 0, :], gs["x1_ready"])
                    act_rowsum(act, gs, n, 0)
                    act_a2(act, gs, n)
                    act_rstd(act, gs, n * 2 + 2, 1, 2)
                    act_norm(act, gs, n * 2 + 2, 1, Z2, OUT[:, 0, :], gs["out_ready"])
                act.nop()

        def v_residual(v, q, n, rr):
            v.wait_ge(q["ow2_mm"], n + 1)
            v.wait_ge(q["xb_ready"], n + 1)
            nc.vector.tensor_tensor(pair(Z[:]), T2, pair(XB[:, rr, :]), ALU.add).then_inc(q["z_ready"], 1)

        def v_stats(src, k):
            for g in range(G):
                last = nc.vector.bn_stats(st[:, k, g, :], src[:, g * C:(g + 1) * C])
            return last

        def v_moments(k):
            for g in range(G):
                last = nc.vector.bn_aggr(mv[:, k, g, :], st[:, k, g, :])
            return last

        def v_shift(v, q, value, k0, k1):
            v.wait_ge(q["rs_ready"], value)
            nc.vector.scalar_tensor_tensor(shift[:, k0:k1, :], mv[:, k0:k1, :, 0], -1.0, rstd[:, k0:k1, :],
                                           ALU.mult, ALU.mult).then_inc(q["shift_ready"], 1)

        def v_rn(v, q, n):
            v.wait_ge(q["ns_ready"], n + 1)
            nc.vector.reciprocal(rn[:], ns[:]).then_inc(q["rn_ready"], 1)

        def v_scale(v, q, n):
            v.wait_ge(q["rn_ready"], n + 1)
            v.wait_ge(q["out_mm"], n + 1)
            for g in range(G):
                last = nc.vector.scalar_tensor_tensor(U[:, g * C:(g + 1) * C], T4[:, g, :], rn[:, g:g + 1], bL_bc,
                                                      ALU.mult, ALU.add)
            last.then_inc(q["u_ready"], 1)

        def v_leaky(v, q, n):
            v.wait_ge(q["u_ready"], n + 1)
            nc.vector.scalar_tensor_tensor(V[:], U[:], 0.01, U[:], ALU.mult, ALU.max).then_inc(q["v_ready"], 1)

        @block.vector
        def _(v):
            nc.vector.memset(ones[:], 1.0)
            nc.vector.memset(ones_h[:], 1.0)
            nc.vector.memset(flags[:], 0.0)
            nc.vector.memset(news[:], 0.0)
            nc.vector.memset(YT[:, :, :, C + TAB - 1:C + TAB], 0.0)
            nc.vector.memset(EPSC, EPS)
            v.wait_ge(pool_consts, 2)
            nc.vector.tensor_copy(iota[:], iota_i[:])
            nc.vector.tensor_copy(part[:], part_i[:])
            nc.vector.drain()
            nc.vector.tensor_scalar(ident[:], iota[:], part[:, 0:1], None, ALU.is_equal)
            nc.vector.tensor_scalar(upper[:], iota[:], part[:, 0:1], None, ALU.is_gt)
            nc.vector.tensor_scalar(part5[:], part[:], float(MAIN), None, ALU.add)
            v.wait_ge(c_dma, 32)
            nc.vector.tensor_scalar(noff_c, noff_c, -1.0, None, ALU.mult)
            nc.vector.tensor_tensor(coef_c, width_c, width_c, ALU.mult)
            nc.vector.drain()
            nc.vector.reciprocal(coef_c, coef_c)
            nc.vector.drain()
            nc.vector.tensor_scalar(coef_c, coef_c, -0.5, None, ALU.mult).then_inc(v_c1, 1)
            def w0():
                nc.vector.tensor_scalar(FB1L, FB1, LN2, None, ALU.subtract)
                nc.vector.tensor_scalar(OB1L, OB1, LN2, None, ALU.subtract)
                nc.vector.tensor_copy(hsum[:, R:R + 1], FB1)
                nc.vector.tensor_copy(hsum[:, 0:R], fw1T)
                nc.vector.drain()
                nc.vector.tensor_reduce(s0[:, 3:4], hsum[:], AX.X, ALU.add, apply_absolute_value=True)
                nc.vector.tensor_copy(b2_hi[:], b2_bc)
                nc.vector.drain()
                nc.vector.tensor_scalar(flags[:, 7:8], s0[:, 3:4], CLAMP, None, ALU.subtract)
                nc.vector.tensor_tensor(b2_res[:], b2_bc, b2_hi[:], ALU.subtract)
                nc.vector.drain()
                nc.vector.tensor_copy(b2_mid[:], b2_res[:])
                nc.vector.drain()
                nc.vector.tensor_tensor(b2_res[:], b2_res[:], b2_mid[:], ALU.subtract)
                nc.vector.tensor_scalar(b2_sel[:], b2_hi[:], ident[:, 0:1], None, ALU.mult)
                nc.vector.drain()
                nc.vector.scalar_tensor_tensor(b2_sel[:], b2_mid[:], ident[:, 1:2], b2_sel[:], ALU.mult, ALU.add)
                nc.vector.drain()
                nc.vector.scalar_tensor_tensor(b2_sel[:], b2_res[:], ident[:, 2:3], b2_sel[:], ALU.mult, ALU.add)
                nc.vector.drain()
                for t in range(PER):
                    nc.vector.tensor_copy(b2_rows[:, t, :], b2_sel[:])
                v.wait_ge(pe_c1, 1)
                nc.vector.tensor_scalar(s0[:, 0:1], AG[:, 0:1], FB1, CLAMP, ALU.add, ALU.min).then_inc(v_c2, 1)
                v.wait_ge(a_c2, 1)
                nc.vector.scalar_tensor_tensor(s0[:, 3:4], AG[:, 0:1], FB1L, s0[:, 2:3], ALU.add, ALU.max)
                nc.vector.drain()
                nc.vector.tensor_scalar(S2[:, 0:N], ones[:], s0[:, 3:4], None, ALU.mult).then_inc(v_c2, 1)
                v.wait_ge(pe_c2, 1)
                nc.vector.tensor_tensor(W0_bc[:], AG[:, 0:C], b2_bc, ALU.add)
                nc.vector.drain().then_inc(v_setup, 1)

            def times_y(t, r, rr, g):
                v.wait_ge(w_mm[g], t - 1)
                wait(v, scat_mm[g], t - 2)
                y = YT[:, rr, :, 0:C]
                if g != 1:
                    y = YT[:, rr, g, 0:C].unsqueeze(1).broadcast_to([N, PER, C])
                nc.vector.tensor_tensor(P[:, g, :].rearrange("p (t c) -> p t c", t=PER),
                                        Wb[w_bank(r, g)][:].rearrange("p (t c) -> p t c", t=PER), y, ALU.mult).then_inc(p_ready[g], 1)

            def hot(rr, q):
                last = one_hot(nc.vector, q, SV[:, rr, 1, q:q + 1], RC[:, rr, q:q + 1])
                if q % PER == PER - 1:
                    last.then_inc(oh_ready[q // PER], 1)

            def step(t, cyc, r):
                a, b2, c1, n1, c2, n2 = (on(t, k) for k in ("A", "B2", "C1", "N1", "C2", "N2"))
                ra, rb = slot(r), slot(r, 2)
                tab = YT[:, ra, 0:2 * G:2, C:C + TAB]
                ovt = YT[:, ra, 1:2 * G:2, C:C + TAB]
                c, rd = turn(cyc, r, 0, UNROLL)

                if a:
                    v.wait_ge(loadA[rd], c * 32 + 32)
                    nc.vector.scalar_tensor_tensor(KEY[:], pair(ADJ[:, rd, :]), CUTOFF, pair(ADJ[:, rd, :]),
                                                   ALU.is_lt, ALU.mult).then_inc(s["key_ready"], 1)
                if n1:
                    last = v_stats(Z, 0)
                if n2:
                    v.wait_ge(s["z2_ready"], t - 4)
                    last = v_stats(Z2, 1)
                if n1 or n2:
                    last.then_inc(s["st_ready"], 1)
                if a:
                    v.wait_ge(s["key_ready"], t + 1)
                    wait(v, s["agg_mm"], t - 2)
                    nc.vector.tensor_scalar(M0[:, ra, :], ADJ[:, rd, :], 0.0, None, ALU.is_equal).then_inc(s["m0_ready"], 1)
                    for g in range(G):
                        last = nc.vector.max(tab[:, g, 0:8], KEY[:, g, :])
                    last.then_inc(s["top8_ready"], 1)
                if b2:
                    v.wait_ge(s["rc_ready"], t - 1)
                    wait(v, scat_mm[0], t - 2)
                    if a:
                        v.wait_ge(s["top8_ready"], t + 1)
                    hot(rb, 0)
                elif a:
                    nc.vector.drain()
                if a:
                    for g in range(G):
                        last = nc.vector.match_replace(KEY2[:, g, :], tab[:, g, 0:8], KEY[:, g, :], -1.0)
                    last.then_inc(s["key2_ready"], 1)
                    for g in range(G):
                        nc.vector.max_index(IDX[:, g, 0:8], tab[:, g, 0:8], KEY[:, g, :])
                if n1 or n2:
                    if b2:
                        v.wait_ge(s["st_ready"], t - 3)
                        hot(rb, 1)
                    else:
                        nc.vector.drain()
                    if n1:
                        last = v_moments(0)
                    if n2:
                        last = v_moments(1)
                    last.then_inc(s["mv_ready"], 1)
                elif b2:
                    hot(rb, 1)
                if b2:
                    if a:
                        v.wait_ge(s["key2_ready"], t + 1)
                    hot(rb, 2)
                elif a:
                    nc.vector.drain()
                if a:
                    for g in range(G):
                        last = nc.vector.max(tab[:, g, 8:16], KEY2[:, g, :])
                    last.then_inc(s["top16_ready"], 1)
                if b2:
                    hot(rb, 3)
                if a:
                    v.wait_ge(s["top16_ready"], t + 1)
                    nc.vector.tensor_scalar(over[:], tab[:, :, MAIN:16], 0.0, None, ALU.is_gt).then_inc(s["over_ready"], 1)
                if n1 or n2:
                    v_shift(v, s, t - 3, 0 if n1 else 1, 2 if n2 else 1)
                if a:
                    v.wait_ge(s["over_ready"], t + 1)
                    with nc.allow_low_precision(reason="whole numbers up to 11"):
                        nc.vector.tensor_reduce(cnt[:, ra, :], over[:], AX.X, ALU.add).then_inc(s["cnt_ready"], 1)
                if b2:
                    times_y(t, r, rb, 0)
                if a:
                    for g in range(G):
                        last = nc.vector.max_index(IDX[:, g, 8:16], tab[:, g, 8:16], KEY2[:, g, :])
                    last.then_inc(s["idx_ready"], 1)
                    v.wait_ge(s["idx_ready"], t + 1)
                    nc.vector.tensor_copy(tab[:, :, 16:32], IDX[:])
                    nc.vector.tensor_copy(news[:, 1:3], tab[:, :, 15])
                if b2:
                    times_y(t, r, rb, 1)
                if a:
                    v.wait_ge(s["rank_mm"], t + 1)
                    nc.vector.tensor_copy(tab[:, :, 32], RANK).then_inc(s["rank_ready"], 1)
                if b2:
                    wait(v, scat_mm[1], t - 2)
                    hot(rb, 4)
                if a:
                    v.wait_ge(s["rank_ready"], t + 1)
                    nc.vector.tensor_tensor(end[:], tab[:, :, 32], cnt[:, ra, :], ALU.add)
                    for g in range(G):
                        last = nc.vector.tensor_scalar(SELa[:, g, :], iota[:], tab[:, g, 32:33], None, ALU.is_ge)
                    last.then_inc(s["sela_ready"], 1)
                if b2:
                    hot(rb, 5)
                if a:
                    v.wait_ge(s["sela_ready"], t + 1)
                    wait(v, s["gather_mm"], t)
                    for g in range(G):
                        last = nc.vector.scalar_tensor_tensor(SEL[:, g, :], iota[:], end[:, g:g + 1], SELa[:, g, :],
                                                              ALU.is_lt, ALU.mult)
                    last.then_inc(s["sel_ready"], 1)
                    nc.vector.tensor_scalar(news[:, 3:5], end[:], float(N), None, ALU.subtract).then_inc(s["news_ready"], 1)
                if b2:
                    hot(rb, 6)
                    hot(rb, 7)
                if a:
                    for g, q in ((0, 0), (1, 8)):
                        nc.vector.tensor_copy(SV[:, ra, :, q:q + 4],
                                              tab[:, g, 0:32].rearrange("p (k c) -> p k c", k=2)[:, :, 0:4])
                    nc.vector.tensor_copy(SV[:, ra, :, 4:8:2],
                                          tab[:, :, 0:32].rearrange("p g (k c) -> p k g c", k=2)[:, :, :, 4])
                if a or c1:
                    if a:
                        v.wait_ge(s["news_ready"], t + 1)
                        v.wait_ge(s["neg_ready"], t + 1)
                    if c1:
                        v.wait_ge(s["e2_ready"], t - 2)
                    nc.vector.tensor_tensor(flags[:, 0:6], flags[:, 0:6], news[:, 0:6], ALU.max).then_inc(s["flags_ready"], 1)
                if c2:
                    v_rn(v, s, t - 4)
                if b2:
                    times_y(t, r, rb, 2)
                if a:
                    v.wait_ge(s["yo_ready"], t + 1)
                    nc.vector.tensor_scalar(rel[:], ovt[:, :, 32], part5[:, 0:1], -1.0, ALU.subtract, ALU.mult).then_inc(s["rel_ready"], 1)
                if c1:
                    v_residual(v, s, t - 3, slot(r, 3))
                if a:
                    v.wait_ge(s["rel_ready"], t + 1)
                    nc.vector.tensor_tensor(mask[:], iota[:, 0:16].unsqueeze(1).broadcast_to([N, G, 16]),
                                            rel[:].unsqueeze(2).broadcast_to([N, G, 16]), ALU.is_equal).then_inc(s["mask_ready"], 1)
                    v.wait_ge(s["mask_ready"], t + 1)
                    nc.vector.tensor_tensor(picked[:], ovt[:, :, 0:32].rearrange("p g (k c) -> p g k c", k=2),
                                            mask[:].unsqueeze(2).broadcast_to([N, G, 2, 16]), ALU.mult).then_inc(s["picked_ready"], 1)
                if a:
                    v.wait_ge(s["picked_ready"], t + 1)
                    nc.vector.tensor_reduce(SV[:, ra, :, 5:8:2].rearrange("p k g -> p g k"), picked[:],
                                            AX.X, ALU.add).then_inc(s["slots_ready"], 1)
                if c2:
                    v_scale(v, s, t - 4)
                    wait(v, s["z2_ready"], t - 4)
                    v_leaky(v, s, t - 4)
                if isinstance(t, int) and t == 0:
                    w0()

            steps(v, step)

            nc.vector.drain()
            nc.vector.tensor_scalar(flags[:, 5:6], flags[:, 5:6], math.exp(CLAMP), None, ALU.subtract)
            nc.vector.drain()
            nc.vector.tensor_reduce(flag1[:], flags[:], AX.X, ALU.max)
            nc.vector.drain()
            nc.vector.tensor_scalar(flag2[:], flag1[:], 0.0, None, ALU.is_gt).then_inc(flag_v, 1)
            v.wait_ge(flag_pe, 1)
            nc.vector.tensor_scalar(flag_i[:], M[0:1, 0:1], 0.0, None, ALU.is_gt).then_inc(flag_ready, 1)
            v.wait_ge(flag_ready, 1)
            general = v.value_load(flag_i[0:1, 0:1], min_val=0, max_val=1)
            with v.If(general > 0):
                with v.Fori(0, PAIRS) as n:
                    v.wait_ge(g_load, n * 64 + 64)
                    nc.vector.tensor_scalar(g_k[:], ADJ[:, 0, :], 0.1, MAGIC, ALU.mult, ALU.add)
                    nc.vector.drain()
                    nc.vector.tensor_scalar(g_k[:], g_k[:], MAGIC, None, ALU.subtract)
                    nc.vector.drain()
                    nc.vector.scalar_tensor_tensor(g_u[:], g_k[:], -10.0, ADJ[:, 0, :], ALU.mult, ALU.add)
                    nc.vector.drain()
                    nc.vector.tensor_tensor(g_u[:], g_u[:], g_u[:], ALU.mult)
                    nc.vector.drain()
                    nc.vector.tensor_scalar(g_k[:], g_u[:], COS[6], None, ALU.mult)
                    for k in range(5, 0, -1):
                        nc.vector.drain()
                        nc.vector.scalar_tensor_tensor(g_k[:], g_k[:], COS[k], g_u[:], ALU.add, ALU.mult)
                    nc.vector.drain()
                    nc.vector.tensor_scalar(g_k[:], g_k[:], COS[0], None, ALU.add)
                    nc.vector.drain()
                    nc.vector.tensor_tensor(g_k[:], g_k[:], g_k[:], ALU.mult)
                    nc.vector.drain()
                    nc.vector.scalar_tensor_tensor(g_rc[:], ADJ[:, 0, :], CUTOFF, g_k[:], ALU.is_lt, ALU.mult)
                    nc.vector.memset(AGG[:], 0.0)
                    nc.vector.tensor_tensor(pair(XB[:, 0, :]), pair(X[:, 0, :]),
                                            ob2_bc.unsqueeze(1).broadcast_to([N, G, C]), ALU.add).then_inc(gs["xb_ready"], 1)
                    nc.vector.drain()
                    for g in range(G):
                        with v.Fori(0, N // PER) as i:
                            m = n * (G * N // PER) + i + g * (N // PER)
                            nc.vector.tensor_copy(g_val[:], ADJ[:, 0, bass.ds(i * PER + g * N, PER)])
                            nc.vector.tensor_copy(g_w[:], g_rc[:, bass.ds(i * PER + g * N, PER)])
                            nc.vector.tensor_copy(g_idx[:], iota[:, bass.ds(i * PER, PER)])
                            nc.vector.drain()
                            nc.vector.tensor_copy(g_vb[:], g_val[:].unsqueeze(2).broadcast_to([N, PER, 32])).then_inc(gs["pick"], 1)
                            for q in range(PER):
                                one_hot(nc.vector, q, g_idx[:, q:q + 1], g_w[:, q:q + 1])
                            v.wait_ge(gs["h_mm"], m + 1)
                            nc.vector.tensor_scalar(E[:, :, 0:N], H[:, :, 0:N], FB1, CLAMP, ALU.add, ALU.min).then_inc(gs["hm"], 1)
                            v.wait_ge(gs["l"], m + 1)
                            nc.vector.scalar_tensor_tensor(S[:, 0, :, 0:N], H[:, :, 0:N], FB1L, E[:, :, 0:N],
                                                           ALU.add, ALU.max).then_inc(gs["s"], 1)
                            v.wait_ge(gs["y_ready"], n * 2 + (g + 1))
                            v.wait_ge(gs["w_mm"], m + 1)
                            nc.vector.tensor_tensor(P[:, 0, :].rearrange("p (t c) -> p t c", t=PER),
                                                    Wb[0][:].rearrange("p (t c) -> p t c", t=PER),
                                                    YT[:, 0, 0, 0:C].unsqueeze(1).broadcast_to([N, PER, C]), ALU.mult)
                            nc.vector.drain().then_inc(gs["p"], 1)
                            v.wait_ge(gs["scat"], m + 1)
                            nc.vector.tensor_tensor(AGG[:, g * N:(g + 1) * N], AG[:, 0:N], AGG[:, g * N:(g + 1) * N], ALU.add)
                            nc.vector.drain()
                    nc.vector.drain().then_inc(gs["agg"], 1)
                    v.wait_ge(gs["ow1_mm"], n + 1)
                    nc.vector.tensor_scalar(pair(HM[:]), T1, OB1, CLAMP, ALU.add, ALU.min).then_inc(gs["hm_ready"], 1)
                    v.wait_ge(gs["l2_ready"], n + 1)
                    nc.vector.scalar_tensor_tensor(pair(S2[:]), T1, OB1L, pair(L2[:]), ALU.add, ALU.max).then_inc(gs["s2_ready"], 1)
                    v_residual(v, gs, n, 0)
                    nc.vector.drain()
                    v_stats(Z, 0)
                    nc.vector.drain()
                    v_moments(0).then_inc(gs["mv_ready"], 1)
                    v_shift(v, gs, n * 2 + 1, 0, 1)
                    v_rn(v, gs, n)
                    v_scale(v, gs, n)
                    v_leaky(v, gs, n)
                    nc.vector.drain()
                    nc.vector.tensor_tensor(Z2[:], V[:], X1[:, 0, :], ALU.add)
                    nc.vector.drain()
                    v_stats(Z2, 1)
                    nc.vector.drain()
                    v_moments(1).then_inc(gs["mv_ready"], 1)
                    v_shift(v, gs, n * 2 + 2, 1, 2)
                v.nop()

        def mm(o, w, m, start=True, stop=True):
            return nc.tensor.matmul(o, w, m, start=start, stop=stop)

        def pe_ow1(pe, q, n):
            for g in range(G):
                last = mm(T1[:, g, :], ow1s, AGG[:, g * N:(g + 1) * N])
            last.then_inc(q["ow1_mm"], 1)

        def pe_ow2(pe, q, n):
            pe.wait_ge(q["s2_ready"], n + 1)
            for g in range(G):
                last = mm(T2[:, g, :], S2[:, g * N:(g + 1) * N], ow2s)
            last.then_inc(q["ow2_mm"], 1)

        def pe_agg2(pe, q, n, rr, ra):
            pe.wait_ge(q["x1_ready"], n + 1)
            for g in range(G):
                last = mm(T3[:, g, :], X1[:, rr, g * C:(g + 1) * C], ADJ[:, ra, g * N:(g + 1) * N])
            last.then_inc(q["a2_mm"], 1)

        def pe_out(pe, q, n):
            pe.wait_ge(q["a2_ready"], n + 1)
            for g in range(G):
                last = mm(T4[:, g, :], A2[:, g * N:(g + 1) * N], WTs)
            last.then_inc(q["out_mm"], 1)

        def filter_out(rr, g, src, W):
            mm(W, ones_h[:], b2_rows[:].rearrange("p t c -> p (t c)"), stop=False)
            for t in range(PER):
                last = mm(W[:, t * C:(t + 1) * C], src[:, rr, t, g * N:(g + 1) * N], fw2s, start=False, stop=(t == PER - 1))
            return last

        @block.tensor
        def _(pe):
            pe.wait_ge(v_c1, 1)

            def w0():
                pe.wait_ge(a_c1, 1)
                mm(AG[:, 0:1], fw1s[0:R, :], f0[0:R, 1:2]).then_inc(pe_c1, 1)
                pe.wait_ge(v_c2, 2)
                mm(AG[:, 0:C], S2[:, 0:N], fw2s).then_inc(pe_c2, 1)

            def hidden(rr, i0, i1):
                for i in range(i0, i1):
                    last = mm(H[:, i, 0:GROUPS * N], fw1s[32 * i:32 * i + R, :], FT[32 * i:32 * i + R, rr, :])
                return last

            def w_group(t, r, rr, g):
                pe.wait_ge(s["s_ready"], t - 1)
                if g == 2:
                    pe.wait_ge(p_ready[0], t - 1)
                else:
                    wait(pe, p_ready[g + 1], t - 2)
                filter_out(rr, g, S, Wb[w_bank(r, g)][:]).then_inc(w_mm[g], 1)

            def scatter(t, rr, g):
                pe.wait_ge(p_ready[g], t - 1)
                if PER * g + PER - 1 in POOL_HOT:
                    pe.wait_ge(oh_pool, t - 1)
                else:
                    pe.wait_ge(oh_ready[g], t - 1)
                for i in range(PER):
                    q = PER * g + i
                    h = GRAPH_OF[q]
                    if q == MAIN + 1:
                        zeros(t, rr, 0)
                    last = mm(AG[:, h * N:(h + 1) * N], P[:, g, i * C:(i + 1) * C], OH[:, q, :],
                              start=(q in (0, MAIN + 1)), stop=False)
                last.then_inc(scat_mm[g], 1)

            def zeros(t, rr, h):
                return mm(AG[:, h * N:(h + 1) * N], YW0[:, rr, h, :], M0[:, rr, h * N:(h + 1) * N], start=False)

            def step(t, cyc, r):
                r1, r2, r4 = slot(r, 1), slot(r, 2), slot(r, 4)
                if isinstance(t, int) and t == 2:
                    pe.wait_ge(v_setup, 1)
                if on(t, "B2"):
                    w_group(t, r, r2, 0)
                if on(t, "A"):
                    c, ra = turn(cyc, r, 0, UNROLL)
                    pe.wait_ge(loadA[ra], c * 32 + 32)
                    wait(pe, s["sq_ready"], t)
                    for g in range(G):
                        last = mm(M[:, g * C:(g + 1) * C], XT[:, slot(r), g * N:(g + 1) * N], win)
                    last.then_inc(s["y_mm"], 1)
                wait(pe, s["z_ready"], min(t - 3, PAIRS) if isinstance(t, int) else t - 3)
                wait(pe, s["u_ready"], t - 4)
                if on(t, "B1"):
                    pe.wait_ge(s["f_ready"], t)
                    hidden(r1, 0, 2).then_inc(s["h_mm"], 1)
                if on(t, "B2"):
                    w_group(t, r, r2, 1)
                if on(t, "B1"):
                    hidden(r1, 2, PER).then_inc(s["hb_mm"], 1)
                if on(t, "A"):
                    pe.wait_ge(s["cnt_ready"], t + 1)
                    pe.wait_ge(s["y_ready"], t + 1)
                    mm(RANK, upper[:], cnt[:, slot(r), :]).then_inc(s["rank_mm"], 1)
                if on(t, "B2"):
                    wait(pe, s["agg_ready"], t - 2)
                    scatter(t, r2, 0)
                    w_group(t, r, r2, 2)
                if on(t, "B1"):
                    pe.wait_ge(s["e_ready"], t)
                if on(t, "C1"):
                    pe.wait_ge(s["agg_ready"], t - 2)
                    pe_ow1(pe, s, t - 3)
                if on(t, "C2"):
                    pe_agg2(pe, s, t - 4, r4, turn(cyc, r, 4, UNROLL)[1])
                if on(t, "A"):
                    pe.wait_ge(s["sel_ready"], t + 1)
                    pe.wait_ge(s["rank_ready"], t + 1)
                    for g in range(G):
                        last = mm(GO[:, g, :], SEL[:, g, :], YT[:, slot(r), 2 * g, :])
                    last.then_inc(s["gather_mm"], 1)
                if on(t, "C1"):
                    pe_ow2(pe, s, t - 3)
                if on(t, "C2"):
                    pe_out(pe, s, t - 4)
                if on(t, "B2"):
                    pe.wait_ge(s["yw0_ready"], t - 1)
                    pe.wait_ge(s["m0_ready"], t - 1)
                    scatter(t, r2, 1)
                if on(t, "B2"):
                    scatter(t, r2, 2)
                if on(t, "A"):
                    pe.wait_ge(s["yo_ready"], t + 1)
                    pe.wait_ge(s["vb_ready"], t + 1)
                    for g in range(GROUPS):
                        src = VB[:, PER * g:PER * g + PER, :].rearrange("p t r -> p (t r)")
                        last = nc.tensor.transpose(M[:, g * N:(g + 1) * N], src, ident[:])
                    last.then_inc(s["bcast_mm"], 1)
                if on(t, "B2"):
                    zeros(t, r2, 1).then_inc(s["agg_mm"], 1)
                if isinstance(t, int) and t == 0:
                    w0()

            steps(pe, step)

            pe.wait_ge(flag_v, 1)
            mm(M[0:1, 0:1], flag2[:], ones[:, 0:1]).then_inc(flag_pe, 1)
            pe.wait_ge(flag_ready, 1)
            general = pe.value_load(flag_i[0:1, 0:1], min_val=0, max_val=1)
            with pe.If(general > 0):
                with pe.Fori(0, PAIRS) as n:
                    pe.wait_ge(g_load, n * 64 + 64)
                    for g in range(G):
                        mm(M[:, 0:C], XT[:, 0, g * N:(g + 1) * N], win).then_inc(gs["y_mm"], 1)
                        with pe.Fori(0, N // PER) as i:
                            m = n * (G * N // PER) + i + g * (N // PER)
                            pe.wait_ge(gs["pick"], m + 1)
                            pe.wait_ge(gs["y_ready"], n * 2 + (g + 1))
                            nc.tensor.transpose(M[:, 0:N], g_vb[:].rearrange("p t r -> p (t r)"), ident[:]).then_inc(gs["bcast"], 1)
                            pe.wait_ge(gs["f"], m + 1)
                            for k in range(PER):
                                last = mm(H[:, k, 0:N], fw1s[32 * k:32 * k + R, :], FT[32 * k:32 * k + R, 0, 0:N])
                            last.then_inc(gs["h_mm"], 1)
                            pe.wait_ge(gs["s"], m + 1)
                            filter_out(0, 0, S, Wb[0][:]).then_inc(gs["w_mm"], 1)
                            pe.wait_ge(gs["p"], m + 1)
                            for k in range(PER):
                                last = mm(AG[:, 0:N], P[:, 0, k * C:(k + 1) * C], OH[:, k, :], start=(k == 0), stop=(k == PER - 1))
                            last.then_inc(gs["scat"], 1)
                    pe.wait_ge(gs["agg"], n + 1)
                    pe_ow1(pe, gs, n)
                    pe_ow2(pe, gs, n)
                    pe_agg2(pe, gs, n, 0, 0)
                    pe_out(pe, gs, n)
                pe.nop()


def kernel(**inputs):
    import numpy as _np
    import concourse.bacc as _bacc
    from concourse import mybir as _mybir
    from concourse.bass_utils import run_bass_kernel_spmd as _run

    def pairs(a):
        return a.reshape(PAIRS, G, N, N).transpose(0, 2, 1, 3).reshape(PAIRS, N, G * N)

    def col(a):
        return a.reshape(-1, 1)

    given = {k.replace("_gnn", ""): _np.asarray(v) for k, v in inputs.items()}
    x, adj, fw1 = given["x"], given["adj"], given["L0_fw1"]

    def strips(a, fill):
        return _np.pad(a, ((0, 32 - R), (0, 0)), constant_values=fill)[None].repeat(N // 32, 0).reshape(N, a.shape[1])

    layouts = {
        "x": pairs(x),
        "xT": pairs(x.transpose(0, 2, 1)),
        "adj": pairs(adj),
        "adjT": pairs(adj.transpose(0, 2, 1)),
        "weights": _np.concatenate([
            given["L0_w_in2f"], given["L0_fw2"], given["L0_ow1"], given["L0_ow2"], given["L1_W"].T, strips(fw1, 0),
            col(given["L0_fb1"]), col(given["L0_ob1"]), strips(col(given["L0_widths"]), 1), strips(col(given["L0_offsets"]), 0),
            fw1.T], axis=1),
        "biases": _np.concatenate([given["L0_fb2"], given["L0_ob2"], given["L1_b"]]),
    }
    nc = _bacc.Bacc("TRN2", target_bir_lowering=False, num_devices=1)
    arrays, args = {}, []
    for name, a in layouts.items():
        a = _np.ascontiguousarray(a)
        arrays[f"in_{name}"] = a
        args.append(nc.dram_tensor(f"in_{name}", a.shape, _mybir.dt.from_np(a.dtype), kind="ExternalInput").ap())
    args.append(nc.dram_tensor("result", (PAIRS, N, G * C), _mybir.dt.float32, kind="ExternalOutput").ap())
    build(nc, *args)
    r = _run(nc, [arrays], core_ids=[0])
    got = r.results[0]["result"]
    return _np.ascontiguousarray(got.reshape(PAIRS, N, G, C).transpose(0, 2, 1, 3).reshape(B, N, C))
```
